# Optimizing a Trainium2 kernel written in Bass

```python
import numpy as np
import jax
import jax.numpy as jnp

def _softmax(x, axis=-1):
    return jax.nn.softmax(x, axis=axis)
def _gelu(x):
    return jax.nn.gelu(x, approximate=True)
def _silu(x):
    return jax.nn.silu(x)
def _sigmoid(x):
    return jax.nn.sigmoid(x)
def _layernorm(x, axis=-1, eps=1e-5):
    m = jnp.mean(x, axis=axis, keepdims=True)
    v = jnp.var(x, axis=axis, keepdims=True)
    return (x - m) / jnp.sqrt(v + eps)
def _scatter_add(tgt, idx, src, axis=0):
    return tgt.at[idx].add(src)
def _segment_sum(src, seg, n):
    return jax.ops.segment_sum(src, seg, n)

kernel_name = 'mk_adj_ffn_d2_adj_256_a22094'

def setup_inputs(seed: int = 0):
    np.random.seed(seed)
    _w = jnp.asarray
    def _rec_inputs():
        import jax
        import jax.numpy as jnp
        _gk = jax.random.key(seed)
        x = -0.0002928 + 1 * jax.random.normal(jax.random.fold_in(_gk, 1), (64, 256, 256), jnp.float32)
        _a = jax.random.bernoulli(jax.random.fold_in(_gk, 2), 0.0625, (256, 256))
        adj = _a.astype(jnp.int32)
        return x, adj
    x, adj = _rec_inputs()
    def _L0_gnn_setup():
        import jax, jax.numpy as jnp
        import numpy as np
        ALPHA = 0.2
        NEG_INF = -9000000000000000.0

        def _gat(inp, adj_mask, W, a):
            h = jnp.matmul(inp, W)
            F_ = h.shape[-1]
            f1 = jnp.matmul(h, a[:F_, 0])
            f2 = jnp.matmul(h, a[F_:, 0])
            e = jax.nn.leaky_relu(f1[:, :, None] + f2[:, None, :], ALPHA)
            if adj_mask is not None:
                e = jnp.where(adj_mask[None, :, :] > 0, e, NEG_INF)
            att = jax.nn.softmax(e, axis=2)
            h_prime = jnp.einsum('bij,bjf->bif', att, h)
            return jax.nn.elu(h_prime)
        key = jax.random.key(seed)
        ks = jax.random.split(key, 10)
        B, N, Fin, H, O = (16, 1024, 256, 512, 256)

        def xavier(k, shape):
            fan_in, fan_out = (shape[0], shape[-1])
            bound = 1.414 * np.sqrt(6.0 / (fan_in + fan_out))
            return jax.random.uniform(k, shape, jnp.float32, -bound, bound)
        return {'x': jax.random.normal(ks[0], (B, N, Fin), jnp.float32), 'adj': jax.random.randint(ks[1], (N, N), 0, 2, jnp.int32), 'mlp1_w': xavier(ks[2], (Fin, H)), 'mlp1_b': jnp.zeros((H,), jnp.float32), 'mlp2_w': xavier(ks[3], (H, O)), 'mlp2_b': jnp.zeros((O,), jnp.float32), 'W_fc': xavier(ks[4], (H, H)), 'a_fc': xavier(ks[5], (2 * H, 1)), 'W_hand': xavier(ks[6], (O, O)), 'a_hand': xavier(ks[7], (2 * O, 1))}
    _L0_gnn_all = _L0_gnn_setup()
    _L0_gnn_in = {k: v for k, v in _L0_gnn_all.items() if k in ('mlp1_w', 'mlp1_b', 'mlp2_w', 'mlp2_b', 'W_fc', 'a_fc', 'W_hand', 'a_hand', )}
    del _L0_gnn_all

    def _L0_ffn_setup():
        import jax, jax.numpy as jnp
        import numpy as np
        B, S, D = (8, 4096, 256)
        H = 4 * D
        CAPACITY = 0.5
        key = jax.random.key(seed)
        ks = jax.random.split(key, 6)
        x = jax.random.normal(ks[0], (B, S, D), dtype=jnp.float32)
        attention_mask = jnp.zeros((B, 1, 1, S), dtype=jnp.float32)
        wr = jax.random.normal(ks[1], (D, 1), dtype=jnp.float32) * 0.02
        br = jnp.zeros((1,), dtype=jnp.float32)
        w1 = jax.random.normal(ks[2], (D, H), dtype=jnp.float32) * 0.02
        b1 = jnp.zeros((H,), dtype=jnp.float32)
        w2 = jax.random.normal(ks[3], (H, D), dtype=jnp.float32) * 0.02
        b2 = jnp.zeros((D,), dtype=jnp.float32)
        return {'x': x, 'attention_mask': attention_mask, 'wr': wr, 'br': br, 'w1': w1, 'b1': b1, 'w2': w2, 'b2': b2}
    _L0_ffn_all = _L0_ffn_setup()
    _L0_ffn_in = {k: v for k, v in _L0_ffn_all.items() if k in ('attention_mask', 'wr', 'br', 'w1', 'b1', 'w2', 'b2', )}
    del _L0_ffn_all

    def _L1_gnn_setup():
        import jax, jax.numpy as jnp
        import numpy as np
        ALPHA = 0.2
        key = jax.random.key(seed)
        k1, k2, k3, k4 = jax.random.split(key, 4)
        B, N, Din, Dout = (8, 2048, 256, 256)
        h = jax.random.normal(k1, (B, N, Din), dtype=jnp.float32)
        adj = jax.random.randint(k2, (N, N), 0, 2, dtype=jnp.int32)
        w_bound = float(np.sqrt(6.0 / (Din + Dout)))
        a_bound = float(np.sqrt(6.0 / (2 * Dout + 1)))
        W = jax.random.uniform(k3, (Din, Dout), dtype=jnp.float32, minval=-w_bound, maxval=w_bound)
        a = jax.random.uniform(k4, (2 * Dout, 1), dtype=jnp.float32, minval=-a_bound, maxval=a_bound)
        return {'h': h, 'adj': adj, 'W': W, 'a': a}
    _L1_gnn_all = _L1_gnn_setup()
    _L1_gnn_in = {k: v for k, v in _L1_gnn_all.items() if k in ('W', 'a', )}
    del _L1_gnn_all

    def _L1_ffn_setup():
        import jax, jax.numpy as jnp
        import numpy as np
        D_MODEL = 256
        D_STATE = 64
        D_CONV = 4
        EXPAND = 2
        HEADDIM = 64
        D_INNER = EXPAND * D_MODEL
        NHEADS = D_INNER // HEADDIM
        CONV_DIM = D_INNER + 2 * D_STATE
        D_IN_PROJ = 2 * D_INNER + 2 * D_STATE + NHEADS
        CHUNK = 256
        EPS = 1e-05

        def segsum(a):
            T = a.shape[-1]
            cs = jnp.cumsum(a, axis=-1)
            ss = cs[..., :, None] - cs[..., None, :]
            mask = jnp.tril(jnp.ones((T, T), dtype=bool))
            return jnp.where(mask, ss, -jnp.inf)

        def mamba2_block(x, W_in, conv_w, conv_b, dt_bias, A_log, D, norm_w, W_out, W_lin, b_lin):
            Bsz, L, _ = x.shape
            zxbcdt = x @ W_in
            z, xBC, dt = jnp.split(zxbcdt, [D_INNER, D_INNER + CONV_DIM], axis=-1)
            xp = jnp.pad(xBC, ((0, 0), (D_CONV - 1, 0), (0, 0)))
            conv = conv_b + sum((xp[:, k:k + L, :] * conv_w[:, k] for k in range(D_CONV)))
            xBC = jax.nn.silu(conv)
            xh, Bmat, Cmat = jnp.split(xBC, [D_INNER, D_INNER + D_STATE], axis=-1)
            dt = jax.nn.softplus(dt + dt_bias)
            A = -jnp.exp(A_log)
            nc = L // CHUNK
            xh = xh.reshape(Bsz, nc, CHUNK, NHEADS, HEADDIM)
            Bc = Bmat.reshape(Bsz, nc, CHUNK, D_STATE)
            Cc = Cmat.reshape(Bsz, nc, CHUNK, D_STATE)
            dtc = dt.reshape(Bsz, nc, CHUNK, NHEADS)
            dA = jnp.einsum('bclh,h->bhcl', dtc, A)
            A_cum = jnp.cumsum(dA, axis=-1)
            Lmat = jnp.exp(segsum(dA))
            xdt = xh * dtc[..., None]
            Y_diag = jnp.einsum('bcln,bcsn,bhcls,bcshp->bclhp', Cc, Bc, Lmat, xdt)
            decay_states = jnp.exp(A_cum[..., -1:] - A_cum)
            states = jnp.einsum('bcln,bhcl,bclhp->bchpn', Bc, decay_states, xdt)
            chunk_decay = jnp.exp(A_cum[..., -1])

            def step(h, inp):
                s, d = inp
                return (h * d[..., None, None] + s, h)
            _, prevs = jax.lax.scan(step, jnp.zeros_like(states[:, 0]), (jnp.moveaxis(states, 1, 0), jnp.moveaxis(chunk_decay, 2, 0)))
            prevs = jnp.moveaxis(prevs, 0, 1)
            Y_off = jnp.einsum('bcln,bchpn,bhcl->bclhp', Cc, prevs, jnp.exp(A_cum))
            Y = (Y_diag + Y_off + xh * D[:, None]).reshape(Bsz, L, D_INNER)
            Y = Y * jax.nn.silu(z)
            Y = Y * jax.lax.rsqrt(jnp.mean(Y * Y, axis=-1, keepdims=True) + EPS) * norm_w
            out = Y @ W_out
            return out @ W_lin + b_lin
        key = jax.random.key(seed)
        ks = jax.random.split(key, 12)
        B, L = (8, 4096)

        def gauss(k, shape, scale):
            return jax.random.normal(k, shape, dtype=jnp.float32) * scale
        return {'x': gauss(ks[0], (B, L, D_MODEL), 1.0), 'W_in': gauss(ks[1], (D_MODEL, D_IN_PROJ), D_MODEL ** (-0.5)), 'conv_w': gauss(ks[2], (CONV_DIM, D_CONV), 0.3), 'conv_b': gauss(ks[3], (CONV_DIM,), 0.1), 'dt_bias': jax.random.uniform(ks[4], (NHEADS,), minval=-4.0, maxval=-1.0), 'A_log': jnp.log(jax.random.uniform(ks[5], (NHEADS,), minval=1.0, maxval=16.0)), 'D': jnp.ones((NHEADS,), jnp.float32), 'norm_w': jnp.ones((D_INNER,), jnp.float32), 'W_out': gauss(ks[6], (D_INNER, D_MODEL), D_INNER ** (-0.5)), 'W_lin': gauss(ks[7], (D_MODEL, D_MODEL), D_MODEL ** (-0.5)), 'b_lin': jnp.zeros((D_MODEL,), jnp.float32)}
    _L1_ffn_all = _L1_ffn_setup()
    _L1_ffn_in = {k: v for k, v in _L1_ffn_all.items() if k in ('W_in', 'conv_w', 'conv_b', 'dt_bias', 'A_log', 'D', 'norm_w', 'W_out', 'W_lin', 'b_lin', )}
    del _L1_ffn_all

    return {
        "x": x,
        "adj": adj,
        "L0_gnn_mlp1_w": _L0_gnn_in["mlp1_w"],
        "L0_gnn_mlp1_b": _L0_gnn_in["mlp1_b"],
        "L0_gnn_mlp2_w": _L0_gnn_in["mlp2_w"],
        "L0_gnn_mlp2_b": _L0_gnn_in["mlp2_b"],
        "L0_gnn_W_fc": _L0_gnn_in["W_fc"],
        "L0_gnn_a_fc": _L0_gnn_in["a_fc"],
        "L0_gnn_W_hand": _L0_gnn_in["W_hand"],
        "L0_gnn_a_hand": _L0_gnn_in["a_hand"],
        "L0_ffn_attention_mask": _L0_ffn_in["attention_mask"],
        "L0_ffn_wr": _L0_ffn_in["wr"],
        "L0_ffn_br": _L0_ffn_in["br"],
        "L0_ffn_w1": _L0_ffn_in["w1"],
        "L0_ffn_b1": _L0_ffn_in["b1"],
        "L0_ffn_w2": _L0_ffn_in["w2"],
        "L0_ffn_b2": _L0_ffn_in["b2"],
        "L1_gnn_W": _L1_gnn_in["W"],
        "L1_gnn_a": _L1_gnn_in["a"],
        "L1_ffn_W_in": _L1_ffn_in["W_in"],
        "L1_ffn_conv_w": _L1_ffn_in["conv_w"],
        "L1_ffn_conv_b": _L1_ffn_in["conv_b"],
        "L1_ffn_dt_bias": _L1_ffn_in["dt_bias"],
        "L1_ffn_A_log": _L1_ffn_in["A_log"],
        "L1_ffn_D": _L1_ffn_in["D"],
        "L1_ffn_norm_w": _L1_ffn_in["norm_w"],
        "L1_ffn_W_out": _L1_ffn_in["W_out"],
        "L1_ffn_W_lin": _L1_ffn_in["W_lin"],
        "L1_ffn_b_lin": _L1_ffn_in["b_lin"],
    }

def reference(x, adj, L0_gnn_mlp1_w, L0_gnn_mlp1_b, L0_gnn_mlp2_w, L0_gnn_mlp2_b, L0_gnn_W_fc, L0_gnn_a_fc, L0_gnn_W_hand, L0_gnn_a_hand, L0_ffn_attention_mask, L0_ffn_wr, L0_ffn_br, L0_ffn_w1, L0_ffn_b1, L0_ffn_w2, L0_ffn_b2, L1_gnn_W, L1_gnn_a, L1_ffn_W_in, L1_ffn_conv_w, L1_ffn_conv_b, L1_ffn_dt_bias, L1_ffn_A_log, L1_ffn_D, L1_ffn_norm_w, L1_ffn_W_out, L1_ffn_W_lin, L1_ffn_b_lin):
    import jax
    import jax.numpy as jnp
    def _L0_gnn_ref(x, adj, mlp1_w, mlp1_b, mlp2_w, mlp2_b, W_fc, a_fc, W_hand, a_hand):
        import jax, jax.numpy as jnp
        import numpy as np
        ALPHA = 0.2
        NEG_INF = -9000000000000000.0

        def _gat(inp, adj_mask, W, a):
            h = jnp.matmul(inp, W)
            F_ = h.shape[-1]
            f1 = jnp.matmul(h, a[:F_, 0])
            f2 = jnp.matmul(h, a[F_:, 0])
            e = jax.nn.leaky_relu(f1[:, :, None] + f2[:, None, :], ALPHA)
            if adj_mask is not None:
                e = jnp.where(adj_mask[None, :, :] > 0, e, NEG_INF)
            att = jax.nn.softmax(e, axis=2)
            h_prime = jnp.einsum('bij,bjf->bif', att, h)
            return jax.nn.elu(h_prime)
        out = jax.nn.relu(jnp.matmul(x, mlp1_w) + mlp1_b)
        residual = out
        out = _gat(jax.nn.relu(out), None, W_fc, a_fc)
        out = jax.nn.elu(out) + residual
        out = jax.nn.relu(jnp.matmul(out, mlp2_w) + mlp2_b)
        residual = out
        out = _gat(jax.nn.relu(out), adj, W_hand, a_hand)
        out = jax.nn.elu(out) + residual
        return jax.nn.relu(out)

    def _L0_ffn_ref(x, attention_mask, wr, br, w1, b1, w2, b2):
        import jax, jax.numpy as jnp
        import numpy as np
        B, S, D = (8, 4096, 256)
        H = 4 * D
        CAPACITY = 0.5
        b, s, d = x.shape
        weights = (jnp.einsum('bsd,do->bso', x, wr) + br)[..., 0]
        k = max(1, int(CAPACITY * s))
        kk = k - 1 if k > 1 else 1
        _, idx = jax.lax.top_k(weights, k)
        sel_idx = idx[:, :kk]
        sel = jnp.take_along_axis(x, sel_idx[:, :, None], axis=1)
        h = jax.nn.gelu(jnp.einsum('bkd,dh->bkh', sel, w1) + b1)
        y = jnp.einsum('bkh,hd->bkd', h, w2) + b2
        w_sel = jnp.take_along_axis(weights, sel_idx, axis=1)
        y = y * w_sel[..., None]
        batch_idx = jnp.arange(b)[:, None]
        processed = jnp.zeros_like(x).at[batch_idx, sel_idx].set(y)
        return processed + x

    def _L1_gnn_ref(h, adj, W, a):
        import jax, jax.numpy as jnp
        import numpy as np
        ALPHA = 0.2
        Wh = jnp.matmul(h, W)
        D = W.shape[1]
        e_src = jnp.matmul(Wh, a[:D])
        e_dst = jnp.matmul(Wh, a[D:])
        e = e_src + jnp.swapaxes(e_dst, 1, 2)
        e = jnp.where(e > 0, e, ALPHA * e)
        mask = (adj > 0)[None, :, :]
        e = jnp.where(mask, e, -jnp.inf)
        alpha_w = jax.nn.softmax(e, axis=-1)
        h_prime = jnp.matmul(alpha_w, Wh)
        return jax.nn.elu(h_prime)

    def _L1_ffn_ref(x, W_in, conv_w, conv_b, dt_bias, A_log, D, norm_w, W_out, W_lin, b_lin):
        import jax, jax.numpy as jnp
        import numpy as np
        D_MODEL = 256
        D_STATE = 64
        D_CONV = 4
        EXPAND = 2
        HEADDIM = 64
        D_INNER = EXPAND * D_MODEL
        NHEADS = D_INNER // HEADDIM
        CONV_DIM = D_INNER + 2 * D_STATE
        D_IN_PROJ = 2 * D_INNER + 2 * D_STATE + NHEADS
        CHUNK = 256
        EPS = 1e-05

        def segsum(a):
            T = a.shape[-1]
            cs = jnp.cumsum(a, axis=-1)
            ss = cs[..., :, None] - cs[..., None, :]
            mask = jnp.tril(jnp.ones((T, T), dtype=bool))
            return jnp.where(mask, ss, -jnp.inf)

        def mamba2_block(x, W_in, conv_w, conv_b, dt_bias, A_log, D, norm_w, W_out, W_lin, b_lin):
            Bsz, L, _ = x.shape
            zxbcdt = x @ W_in
            z, xBC, dt = jnp.split(zxbcdt, [D_INNER, D_INNER + CONV_DIM], axis=-1)
            xp = jnp.pad(xBC, ((0, 0), (D_CONV - 1, 0), (0, 0)))
            conv = conv_b + sum((xp[:, k:k + L, :] * conv_w[:, k] for k in range(D_CONV)))
            xBC = jax.nn.silu(conv)
            xh, Bmat, Cmat = jnp.split(xBC, [D_INNER, D_INNER + D_STATE], axis=-1)
            dt = jax.nn.softplus(dt + dt_bias)
            A = -jnp.exp(A_log)
            nc = L // CHUNK
            xh = xh.reshape(Bsz, nc, CHUNK, NHEADS, HEADDIM)
            Bc = Bmat.reshape(Bsz, nc, CHUNK, D_STATE)
            Cc = Cmat.reshape(Bsz, nc, CHUNK, D_STATE)
            dtc = dt.reshape(Bsz, nc, CHUNK, NHEADS)
            dA = jnp.einsum('bclh,h->bhcl', dtc, A)
            A_cum = jnp.cumsum(dA, axis=-1)
            Lmat = jnp.exp(segsum(dA))
            xdt = xh * dtc[..., None]
            Y_diag = jnp.einsum('bcln,bcsn,bhcls,bcshp->bclhp', Cc, Bc, Lmat, xdt)
            decay_states = jnp.exp(A_cum[..., -1:] - A_cum)
            states = jnp.einsum('bcln,bhcl,bclhp->bchpn', Bc, decay_states, xdt)
            chunk_decay = jnp.exp(A_cum[..., -1])

            def step(h, inp):
                s, d = inp
                return (h * d[..., None, None] + s, h)
            _, prevs = jax.lax.scan(step, jnp.zeros_like(states[:, 0]), (jnp.moveaxis(states, 1, 0), jnp.moveaxis(chunk_decay, 2, 0)))
            prevs = jnp.moveaxis(prevs, 0, 1)
            Y_off = jnp.einsum('bcln,bchpn,bhcl->bclhp', Cc, prevs, jnp.exp(A_cum))
            Y = (Y_diag + Y_off + xh * D[:, None]).reshape(Bsz, L, D_INNER)
            Y = Y * jax.nn.silu(z)
            Y = Y * jax.lax.rsqrt(jnp.mean(Y * Y, axis=-1, keepdims=True) + EPS) * norm_w
            out = Y @ W_out
            return out @ W_lin + b_lin
        return mamba2_block(x, W_in, conv_w, conv_b, dt_bias, A_log, D, norm_w, W_out, W_lin, b_lin)

    x = x + _L0_gnn_ref(_layernorm(x, axis=-1), adj, L0_gnn_mlp1_w, L0_gnn_mlp1_b, L0_gnn_mlp2_w, L0_gnn_mlp2_b, L0_gnn_W_fc, L0_gnn_a_fc, L0_gnn_W_hand, L0_gnn_a_hand)
    x = x + _L0_ffn_ref(_layernorm(x, axis=-1), L0_ffn_attention_mask, L0_ffn_wr, L0_ffn_br, L0_ffn_w1, L0_ffn_b1, L0_ffn_w2, L0_ffn_b2)
    x = x + _L1_gnn_ref(_layernorm(x, axis=-1), adj, L1_gnn_W, L1_gnn_a)
    x = x + _L1_ffn_ref(_layernorm(x, axis=-1), L1_ffn_W_in, L1_ffn_conv_w, L1_ffn_conv_b, L1_ffn_dt_bias, L1_ffn_A_log, L1_ffn_D, L1_ffn_norm_w, L1_ffn_W_out, L1_ffn_W_lin, L1_ffn_b_lin)
    return x


_drawn_inputs = setup_inputs


def setup_inputs(seed=0):
    import zlib

    import numpy as np

    out = dict(_drawn_inputs(seed))
    spreads = {'L0_gnn_mlp1_b': (0.0, 0.1),
     'L0_gnn_mlp2_b': (0.0, 0.1),
     'L0_ffn_b1': (0.0, 0.8),
     'L0_ffn_b2': (0.0, 0.8),
     'L1_ffn_D': (1.0, 0.6),
     'L1_ffn_norm_w': (1.0, 0.6),
     'L1_ffn_b_lin': (0.0, 1.027)}
    factors = {'L0_ffn_wr': 8.0,
     'L0_ffn_w1': 8.0,
     'L0_ffn_w2': 8.0,
     'L1_gnn_a': 3.643,
     'L1_ffn_A_log': 26.936,
     'L1_ffn_conv_b': 3.991,
     'L1_ffn_dt_bias': 5.88}
    for name, (base, spread) in spreads.items():
        noise = np.random.default_rng([zlib.crc32(name.encode()), seed]).standard_normal(out[name].shape)
        drawn = base * np.exp(spread * noise) if base else spread * noise
        out[name] = jnp.asarray(drawn.astype(out[name].dtype))
    for name, factor in factors.items():
        out[name] = (out[name] * factor).astype(out[name].dtype)
    return out
```

```python
from contextlib import ExitStack

import numpy as np

import concourse.bass as bass
from concourse import mybir

ALU = mybir.AluOpType
ACT = mybir.ActivationFunctionType
F32 = mybir.dt.float32
I32 = mybir.dt.int32
AX_X = mybir.AxisListType.X

P = 128
EPS = 1e-5
ALPHA = 0.2
NEG = 9.0e15
GELU_CUBE = 0.044715
GELU_SCALE = 0.7978845608028654

STEPS = [
    ("b_x1", 1), ("m_turn", 3), ("a_load", 0), ("g_att", 2), ("m_xbc_a", 3), ("q_stats", 1), ("a_stats", 0),
    ("g_elu_a", 2), ("q_norm", 1), ("m_xbc_b", 3), ("a_norm", 0), ("g_elu_b", 2), ("m_dt", 3), ("q_turn", 1),
    ("a_turn", 0), ("q_route", 1), ("a_mlp1", 0), ("q_route_col", 1), ("q_rank", 1), ("m_dt_exp", 3),
    ("m_conv_a", 3), ("m_dt_log", 3), ("q_select", 1), ("m_conv_b", 3), ("q_gather", 1), ("a_fc", 0),
    ("a_fcol", 0), ("m_da", 3), ("g_x3", 2), ("a_bcast", 0), ("a_maxima", 0), ("m_scan", 3), ("m_silu", 3),
    ("a_factors", 0), ("q_ffn1", 1), ("m_stats", 2), ("q_gelu_a", 1), ("m_z", 3), ("a_probs", 0),
    ("q_gelu_b", 1), ("m_gate", 3), ("m_cum_col", 3), ("q_gelu_c", 1), ("m_spread", 3), ("a_att", 0),
    ("a_elu_a", 0), ("q_ffn2", 1), ("a_elu_b", 0), ("m_decay", 3), ("q_scatter", 1), ("a_elu_c", 0),
    ("m_cb", 3), ("a_uturn", 0), ("q_x2", 1), ("g_stats", 1), ("g_norm", 1), ("m_mix", 3), ("m_xrow", 3),
    ("a_mlp2", 0), ("g_turn", 1), ("b_proj", 0), ("g_proj", 1), ("b_bcast", 0), ("b_mask", 0), ("b_lrelu", 0),
    ("b_max", 0), ("m_y", 3), ("g_bcast", 1), ("g_mask", 1), ("b_exp", 0), ("b_pturn", 0), ("g_lrelu", 1),
    ("a_residual", 0), ("m_yturn", 3), ("m_gated", 3), ("m_norm", 2), ("g_max", 1), ("g_exp", 1), ("m_rms", 3),
    ("b_att", 0), ("m_out", 3), ("b_elu_a", 0), ("g_pturn", 1), ("b_elu_b", 0), ("m_store", 3), ("b_elu_c", 0),
]


def log1p_coefficients(degree):
    nodes = (1 + np.cos(np.pi * (np.arange(64) + 0.5) / 64)) / 18
    root = np.sqrt(nodes)
    return [float(c) for c in np.polynomial.polynomial.polyfit(nodes, np.arctanh(root) / root, degree)]


def gnn_ffn_mamba_kernel(nc, x, adj, mlp1_w, mlp1_b, mlp2_w, mlp2_b, W_fc, a_fc, W_hand, a_hand,
                         wr, br, w1, b1, w2, b2, gW, ga, W_in, conv_w, conv_b, dt_bias, A_log, D_skip,
                         norm_w, W_out, W_lin, b_lin, out):
    B, N, D = x.shape
    H = mlp1_w.shape[1]
    F = w1.shape[1]
    DI = W_out.shape[0]
    NH = D_skip.shape[0]
    HD = DI // NH
    DS = (conv_w.shape[0] - DI) // 2
    TAPS = conv_w.shape[1]
    U = N // P
    KD = D // P
    KH = H // P
    KF = F // P
    KI = DI // P
    KX = KI + 1
    TOPK = max(1, int(0.5 * N)) - 1
    PAD = TAPS - 1
    Z0, X0, DT0 = 0, DI, 2 * DI + 2 * DS
    assert U == 2 and KD == 2 and KH == 4 and KI == 4 and 2 * DS == P and TOPK < P and TAPS == 4
    LOG = log1p_coefficients(4)

    with ExitStack() as ctx:
        def sb(name, shape, dt=F32):
            return ctx.enter_context(nc.sbuf_tensor(name, shape, dt))

        def bank(name):
            return ctx.enter_context(nc.psum_tensor(name, [P, 512], F32))

        def sem(name):
            return ctx.enter_context(nc.semaphore(name))

        w_mlp1 = sb("w_mlp1", [P, KD, H])
        c_mlp1 = sb("c_mlp1", [P, KH])
        w_fc = sb("w_fc", [P, KH, H])
        w_mlp2 = sb("w_mlp2", [P, KH, D])
        c_mlp2 = sb("c_mlp2", [P, KD])
        w_hand = sb("w_hand", [P, KD, D])
        w_gat = sb("w_gat", [P, KD, D])
        w_route = sb("w_route", [P, KD])
        w_route_b = sb("w_route_b", [P, KD, P])
        c_route = sb("c_route", [P, 1])
        w_up = sb("w_up", [P, KD, F])
        c_up = sb("c_up", [P, KF])
        w_down = sb("w_down", [P, KF, D])
        c_down = sb("c_down", [P, D])
        w_in = sb("w_in", [P, KD, W_in.shape[1]])
        w_conv = sb("w_conv", [P, KX, TAPS])
        c_conv = sb("c_conv", [P, KX])
        c_dt = sb("c_dt", [P, U, NH])
        a_row = sb("a_row", [P, U, NH])
        d_col = sb("d_col", [P, KI])
        d_diag = sb("d_diag", [P, KI, P])
        n_col = sb("n_col", [P, KI])
        w_comb = sb("w_comb", [P, KI, D])
        c_lin = sb("c_lin", [P, D])
        v_fc = sb("v_fc", [P, KH, 2])
        v_hand = sb("v_hand", [P, KD, 2])
        v_gat = sb("v_gat", [P, KD, 2])
        ident = sb("ident", [P, P])
        ones = sb("ones", [P, N])
        causal = sb("causal", [P, N + P])
        earlier = sb("earlier", [P, U, N])
        slot_i = sb("slot_i", [P, P], I32)
        slot = sb("slot", [P, P])
        power = sb("power", [P, U])
        epsilon = sb("epsilon", [P, U])
        gate_cols = sb("gate_cols", [P, 32])
        hold_cols = sb("hold_cols", [P, 4])
        inverse = sb("inverse", [P, U * NH])
        twos = sb("twos", [P, U * NH])
        log_c = sb("log_c", [P, len(LOG), U * NH])
        mask0 = sb("mask0", [P, U, N])
        mask1 = sb("mask1", [P, U, N])

        x_in = sb("x_in", [P, U, D])
        x0 = sb("x0", [P, U, D])
        x1 = sb("x1", [P, U, D])
        x2 = sb("x2", [P, U, D])
        x3 = sb("x3", [P, U, D])
        x4 = sb("x4", [P, U, D])
        bn = {k: sb(f"bn_{k}", [P, U, 6]) for k in "aqgm"}
        mv = {k: sb(f"mv_{k}", [P, U, 2]) for k in "aqgm"}
        var = {k: sb(f"var_{k}", [P, U]) for k in "aqgm"}
        rstd = {k: sb(f"rstd_{k}", [P, U]) for k in "aqgm"}
        xn = {k: sb(f"xn_{k}", [P, U, D]) for k in "aqgm"}
        xT = {k: sb(f"xT_{k}", [P, KD, N]) for k in "aqgm"}

        o1T = sb("o1T", [P, KH, N])
        h1 = sb("h1", [P, U, H])
        f1 = sb("f1", [P, U, 2])
        top = sb("top", [P, 1])
        arg = sb("arg", [P, N])
        fac = sb("fac", [P, 2, N])
        args = fac
        gcol = sb("gcol", [P, U])
        bcol = sb("bcol", [P, U])
        dcol = sb("dcol", [P, U])
        low = sb("low", [P, U, N])
        p1 = low
        r1 = sb("r1", [P, U])
        e1 = sb("e1", [P, U, H])
        e1m = e1x = e1
        u1 = sb("u1", [P, U, H])
        z1T = e1[:, :, :].rearrange("p u (h n) -> p (u h) n", n=N)
        o2T = sb("o2T", [P, KD, N])

        hp = {k: sb(f"hp_{k}", [P, U, D]) for k in "bg"}
        fc = {k: sb(f"fc_{k}", [P, U, 2]) for k in "bg"}
        sc = {k: sb(f"sc_{k}", [P, U, N]) for k in "bg"}
        nmax = {k: sb(f"nmax_{k}", [P, U]) for k in "bg"}
        lr = pr = sc
        rs = {k: sb(f"rs_{k}", [P, U]) for k in "bg"}
        rr = {k: sb(f"rr_{k}", [P, U]) for k in "bg"}
        pT = {k: sb(f"pT_{k}", [P, U, N]) for k in "bg"}
        ea = {k: sb(f"ea_{k}", [P, U, D]) for k in "bg"}
        eb = ea
        ec = ea["b"]
        ue = {k: sb(f"ue_{k}", [P, U, D]) for k in "bg"}
        v1 = ue["b"]

        wrow = sb("wrow", [P, N])
        wcol = sb("wcol", [P, U])
        junk = sb("junk", [P, N])
        above = sb("above", [P, U])
        ties = sb("ties", [P, U])
        rank = sb("rank", [P, U])
        pick = sb("pick", [P, U, P])
        pickT = sb("pickT", [P, N])
        selT = sb("selT", [P, KD, P])
        ga_ = sb("ga_", [P, KF, P])
        gsq = sb("gsq", [P, KF, P])
        gpl = gq = gt = gl = gsq
        yff = sb("yff", [P, D])
        xs = sb("xs", [P, U, D])

        xbc = sb("xbc", [P, KX, PAD + N])
        acc = sb("acc", [P, KX, N])
        th = sb("th", [P, KX, N])
        xc = acc
        bT = sb("bT", [DS, N])
        cT = sb("cT", [DS, N])
        dt_raw = sb("dt_raw", [P, U * NH])
        dt_a = sb("dt_a", [P, U * NH])
        dt_e = sb("dt_e", [P, U * NH])
        dt_p = sb("dt_p", [P, U * NH])
        dt_w = [sb(f"dt_w{i}", [P, U * NH]) for i in range(14)]
        dt = sb("dt", [P, U, NH])
        dt8 = sb("dt8", [P, U, NH])
        dA = sb("dA", [P, U, NH])
        cumT = sb("cumT", [P, N])
        cumcol = sb("cumcol", [P, U, NH])
        cumB = sb("cumB", [P, NH, N])
        dec0 = sb("dec0", [P, NH, N])
        dec1 = sb("dec1", [P, NH, P])
        cb = sb("cb", [P, N + P])
        tz = sb("tz", [P, U, DI])
        gz = yg = tz
        xdt = sb("xdt", [P, U, DI])
        ysq = th[:, 0:KI, :].rearrange("p (u h) n -> p u (h n)", u=U)
        ss = sb("ss", [P, U])
        ms = sb("ms", [P, U])
        rms = sb("rms", [P, U])
        ygT = xdt[:, :, :].rearrange("p u (h n) -> p (u h) n", n=N)
        x3b = sb("x3b", [P, U, D])
        cum_dram = nc.dram_tensor("cum_dram", [NH, N], F32, kind="Internal").ap()

        A0, A1, A2 = bank("A0"), bank("A1"), bank("A2")
        Q0, Q1 = bank("Q0"), bank("Q1")
        M0, M1, M2 = bank("M0"), bank("M1"), bank("M2")

        def two(b):
            return b[:, :].rearrange("p (u n) -> p u n", u=2)

        NAMES = """a_stats a_rstd a_xn a_xT_ps a_xT  q_stats q_rstd q_xn q_xT_ps q_xT
            g_stats g_rstd g_xn g_xT_ps g_xT  m_stats m_rstd m_xn m_xT_ps m_xT
            o1_ps o1_ready h1_ps h1_a h1_b f1_ps f1_ready fb_ps top_ready gcol_ready
            arg_ready args_ready fac_ready bd_ready low_ready p1_ready y1_ps s1_ps r1_ready e1_ready e1m_ready
            e1x_ready u1_ready u1T_ps z1_ready o2_ps o2_ready x1_ready
            b_h_ps b_f_ps b_hp b_fc b_fb_ps b_sc b_lr b_nmax b_pr b_pT_ps b_pT b_rr b_y_ps b_ea b_eb b_ec b_ue
            res_ps v1_ready
            g_h_ps g_f_ps g_hp g_fc g_fb_ps g_sc g_lr g_nmax g_pr g_pT_ps g_pT g_rr g_y_ps g_ea g_eb g_ue
            w_ps wrow_ready wcol_ready counts_ready rank_ready pick_ready pickT_ps pickT_ready sel_ps sel_ready
            up_ps ga_ready gsq_ready gpl_ready gq_ready gt_ready gl_ready yff_ps yff_ready sc_ps xs_ready
            x2_ready x3_ready
            xbc_ps xbc_ready acc_ready conv th_ready xc_ready
            dt_copied dt_a_ready dt_abs dt_e_ready dt_chain dt_ready dA_ps cumT_ready cumc_ps cumcol_ready
            cb_ps cb_ready z_ps tz_ready gz_ready xr_ps xdt_ready decarg_ready dec_ready mix_ready
            y_ps yg_ready ss_ready da_ready rms_ready yT_ps yT_ready out_ps x3b_ready x4_ready"""
        S = {name: sem(name) for name in NAMES.split()}
        x_loaded = sem("x_loaded")
        x0_loaded = sem("x0_loaded")
        cum_stored = sem("cum_stored")
        cum_spread = sem("cum_spread")
        out_stored = sem("out_stored")
        consts = sem("consts")

        setup_sem = [sem(f"setup{i}") for i in range(5)]
        DV, PL, PEs, AC, LD = setup_sem
        adj_i = xbc[:, 0:2, 0:N]
        adj_f = th[:, 0:2, :]
        a_fc_b = e1
        a_hand_b = u1
        a_gat_b = yg
        w_out_s = dec0[:, 0:KI, 0:D]
        w_outT = dec0[:, KI:KI + KD + 2, 0:D]
        w_lin_s = ygT[:, 0:KD, 0:D]
        a_log_s = dt_a[:, 0:NH]

        with nc.Block() as setup:
            loads = []

            def col(v, k):
                return v.rearrange("(k p) -> p k", p=P)

            def row(v):
                return v.rearrange("(a n) -> a n", a=1).partition_broadcast(P).rearrange("q a n -> q (a n)")

            loads.append((adj_i.bitcast(I32), adj.rearrange("(u p) n -> p u n", p=P)))
            loads.append((w_mlp1[:], mlp1_w.rearrange("(k p) n -> p k n", p=P)))
            loads.append((w_fc[:], W_fc.rearrange("(k p) n -> p k n", p=P)))
            loads.append((w_mlp2[:], mlp2_w.rearrange("(k p) n -> p k n", p=P)))
            loads.append((w_hand[:], W_hand.rearrange("(k p) n -> p k n", p=P)))
            loads.append((w_gat[:], gW.rearrange("(k p) n -> p k n", p=P)))
            loads.append((w_up[:], w1.rearrange("(k p) n -> p k n", p=P)))
            loads.append((w_down[:], w2.rearrange("(k p) n -> p k n", p=P)))
            loads.append((w_in[:], W_in.rearrange("(k p) n -> p k n", p=P)))
            loads.append((w_out_s, W_out.rearrange("(k p) n -> p k n", p=P)))
            loads.append((w_lin_s, W_lin.rearrange("(k p) n -> p k n", p=P)))
            loads.append((w_conv[:], conv_w.rearrange("(k p) t -> p k t", p=P)))
            loads.append((a_fc_b[:], a_fc.rearrange("(s n) o -> (n o) s", s=1).rearrange("n s -> s n")
                          .partition_broadcast(P).rearrange("q s (h n) -> q (s h) n", h=2)))
            loads.append((a_hand_b[:, 0, :], a_hand.rearrange("n o -> o n").partition_broadcast(P)
                          .rearrange("q o n -> q (o n)")))
            loads.append((a_gat_b[:, 0, :], ga.rearrange("n o -> o n").partition_broadcast(P)
                          .rearrange("q o n -> q (o n)")))
            loads.append((w_route[:], wr.rearrange("(k p) o -> p (k o)", p=P)))
            loads.append((c_mlp1[:], col(mlp1_b, KH)))
            loads.append((c_mlp2[:], col(mlp2_b, KD)))
            loads.append((c_up[:], col(b1, KF)))
            loads.append((c_conv[:], col(conv_b, KX)))
            loads.append((n_col[:], col(norm_w, KI)))
            loads.append((c_route[:], row(br)))
            loads.append((c_down[:], row(b2)))
            loads.append((c_lin[:], row(b_lin)))
            for u in range(U):
                loads.append((c_dt[:, u, :], row(dt_bias)))
            loads.append((a_log_s, row(A_log)))
            for half in range(P // HD):
                src = D_skip.rearrange("(k two) -> two k", two=P // HD)[half:half + 1, :]
                loads.append((d_col[half * HD:(half + 1) * HD, :],
                              src.partition_broadcast(HD).rearrange("q a n -> q (a n)")))

            @setup.sync
            def _(sp):
                with nc.allow_non_contiguous_dma("parameters, once"):
                    for dst, src in loads:
                        sp.dma_start(dst, src).then_inc(LD, 16)

            @setup.gpsimd
            def _(pool):
                nc.gpsimd.memset(ident[:], 0.0)
                nc.gpsimd.memset(ones[:], 1.0)
                nc.gpsimd.memset(causal[:], 1.0)
                nc.gpsimd.memset(earlier[:], 1.0)
                nc.gpsimd.memset(power[:], -0.5)
                nc.gpsimd.memset(epsilon[:], EPS)
                nc.gpsimd.memset(inverse[:], -1.0)
                nc.gpsimd.memset(twos[:], 2.0)
                for i, c in enumerate(LOG):
                    nc.gpsimd.memset(log_c[:, i, :], 2.0 * c)
                nc.gpsimd.memset(cumT[:], 0.0)
                nc.gpsimd.iota(slot_i[:], pattern=[[1, P]], base=0, channel_multiplier=0).then_inc(PL, 1)
                pool.wait_ge(PL, 1)
                nc.gpsimd.affine_select(out=ident[:], in_=ident[:], compare_op=ALU.not_equal, fill=1.0, base=0,
                                        pattern=[[-1, P]], channel_multiplier=1)
                nc.gpsimd.affine_select(out=causal[:, 0:N], in_=causal[:, 0:N], compare_op=ALU.is_ge, fill=0.0,
                                        base=0, pattern=[[1, N]], channel_multiplier=-1)
                nc.gpsimd.affine_select(out=causal[:, N:], in_=causal[:, N:], compare_op=ALU.is_ge, fill=0.0,
                                        base=0, pattern=[[1, P]], channel_multiplier=-1)
                nc.gpsimd.affine_select(out=earlier[:], in_=earlier[:], compare_op=ALU.is_gt, fill=0.0, base=0,
                                        pattern=[[P, U], [-1, N]], channel_multiplier=1)
                nc.gpsimd.tensor_copy(slot[:], slot_i[:]).then_inc(PL, 1)
                pool.wait_ge(PL, 2)
                nc.gpsimd.memset(slot[:, TOPK:], -1.0).then_inc(PL, 1)

            @setup.vector
            def _(v):
                n = [0]

                def done(ins):
                    n[0] += 1
                    ins.then_inc(DV, 1)

                def settle():
                    v.wait_ge(DV, n[0])

                v.wait_ge(LD, 16 * len(loads))
                v.wait_ge(PL, 3)
                done(nc.vector.tensor_scalar(adj_f, adj_i.bitcast(I32), 0, None, ALU.is_gt))
                settle()
                done(nc.vector.tensor_scalar(mask0[:], adj_f, -1.0, NEG, ALU.add, ALU.mult))
                settle()
                done(nc.vector.tensor_reduce(rs["g"][:], adj_f, AX_X, ALU.add))
                settle()
                done(nc.vector.reciprocal(rr["g"][:], rs["g"][:]))
                settle()
                done(nc.vector.tensor_scalar(nmax["g"][:], rr["g"][:], 0.0, None, ALU.mult))
                settle()
                for u in range(U):
                    done(nc.vector.tensor_scalar(mask1[:, u, :], mask0[:, u, :], nmax["g"][:, u:u + 1], None, ALU.add))
                for w, k, a_b, v_out, width in ((w_fc, KH, a_fc_b, v_fc, H), (w_hand, KD, a_hand_b, v_hand, D),
                                                (w_gat, KD, a_gat_b, v_gat, D)):
                    for t in range(k):
                        for half in range(2):
                            a_half = a_b[:, half, :] if width == H else a_b[:, 0, half * D:(half + 1) * D]
                            done(nc.vector.scalar_tensor_tensor(
                                out=p1[:, :, :].rearrange("p u n -> p (u n)")[:, 0:width], in0=w[:, t, :],
                                scalar=1.0, in1=a_half, op0=ALU.mult, op1=ALU.mult,
                                accum_out=v_out[:, t, half:half + 1]))
                            settle()
                for t in range(KD):
                    done(nc.vector.tensor_scalar(w_route_b[:, t, :], ones[:, 0:P], w_route[:, t:t + 1], None,
                                                 ALU.mult))
                for t in range(KI):
                    done(nc.vector.tensor_scalar(d_diag[:, t, :], ident[:], d_col[:, t:t + 1], 0.5,
                                                 ALU.mult, ALU.mult))
                done(nc.vector.tensor_scalar(w_down[:], w_down[:], 0.5, None, ALU.mult))
                v.wait_ge(AC, 1)
                for u in range(U):
                    done(nc.vector.tensor_scalar(a_row[:, u, :], dt_e[:, 0:NH], -1.0, None, ALU.mult))
                for m in range(KD):
                    v.wait_ge(PEs, m + 1)
                    done(nc.vector.tensor_copy(w_outT[:, 2 * m:2 * m + 2, :].rearrange("p a n -> p (a n)"),
                                               (A0, A1)[m][:, :]))
                v.wait_ge(PEs, KD + 1)
                for t in range(KI):
                    done(nc.vector.tensor_scalar(w_comb[:, t, :], (M0, M1)[t // 2][:, (t % 2) * D:(t % 2 + 1) * D],
                                                 n_col[:, t:t + 1], None, ALU.mult))
                settle()
                nc.vector.memset(xbc[:, :, 0:PAD], 0.0).then_inc(consts, 1)

            DV_TURNED = 2 + 3 + U + 2 * (KH + KD + KD) + KD + KI + 1 + U + KD

            @setup.scalar
            def _(act):
                act.wait_ge(LD, 16 * len(loads))
                nc.scalar.activation(dt_e[:, 0:NH], a_log_s, ACT.Exp).then_inc(AC, 1)

            @setup.tensor
            def _(pe):
                pe.wait_ge(LD, 16 * len(loads))
                pe.wait_ge(PL, 3)
                for m in range(KD):
                    for t in range(KI):
                        last = nc.tensor.transpose((A0, A1)[m][:, t * P:(t + 1) * P],
                                                   w_out_s[:, t, m * P:(m + 1) * P], ident[:])
                    last.then_inc(PEs, 1)
                pe.wait_ge(DV, DV_TURNED)
                wT = w_outT.rearrange("p (m a) n -> p m (a n)", m=KD)
                for t in range(KI):
                    for m in range(KD):
                        last = nc.tensor.matmul((M0, M1)[t // 2][:, (t % 2) * D:(t % 2 + 1) * D],
                                                wT[:, m, t * P:(t + 1) * P], w_lin_s[:, m, :],
                                                start=(m == 0), stop=(m == KD - 1))
                last.then_inc(PEs, 1)

        def turns(eng, steps):
            last = max(lag for _, lag in STEPS)

            def turn(t):
                for name, lag in STEPS:
                    b = t - lag
                    if name in steps and not (isinstance(b, int) and not 1 <= b <= B):
                        steps[name](b)

            for t in range(1, last + 2):
                turn(t)
            with eng.Fori(last + 2, B + 1) as t:
                turn(t)
            for t in range(B + 1, B + last + 1):
                turn(t)

        def nth(b, per, i):
            return b * per - (per - i)

        def before(eng, semaphore, b):
            if not (isinstance(b, int) and b < 2):
                eng.wait_ge(semaphore, b - 1)

        block = ctx.enter_context(nc.Block())

        @block.sync
        def _(sp):
            def a_load(b):
                before(sp, S["a_xn"], b)
                sp.dma_start(x_in[:], x[b - 1].rearrange("(u p) d -> p u d", p=P)).then_inc(x_loaded, 16)

            def a_residual(b):
                before(sp, S["x1_ready"], b)
                sp.dma_start(x0[:], x[b - 1].rearrange("(u p) d -> p u d", p=P)).then_inc(x0_loaded, 16)

            def m_spread(b):
                sp.wait_ge(S["cumT_ready"], b)
                sp.dma_start(cum_dram, cumT[0:NH, :]).then_inc(cum_stored, 16)
                sp.wait_ge(cum_stored, 16 * b)
                sp.dma_start(cumB[:], cum_dram.partition_broadcast(P)).then_inc(cum_spread, 16)

            def m_store(b):
                sp.wait_ge(S["x4_ready"], b)
                sp.dma_start(out[b - 1].rearrange("(u p) d -> p u d", p=P), x4[:]).then_inc(out_stored, 16)

            turns(sp, dict(a_load=a_load, a_residual=a_residual, m_spread=m_spread, m_store=m_store))
            sp.wait_ge(cum_stored, 16 * B)
            sp.wait_ge(out_stored, 16 * B)

        @block.gpsimd
        def _(pool):
            GATES = {}

            def after(semaphore, b):
                pool.wait_ge(semaphore, b)

            def gate(semaphore, b, part=0):
                after(semaphore, b)
                c = GATES.setdefault((semaphore.name, part), len(GATES))
                nc.gpsimd.tensor_tensor(gate_cols[:, c:c + 1], ones[:, 0:1], ones[:, 0:1], ALU.add)

            def rstd_of(k):
                def step(b):
                    after(S[f"{k}_stats"], nth(b, 2, 2))
                    nc.gpsimd.tensor_tensor(var[k][:], mv[k][:, :, 1], epsilon[:], ALU.add).then_inc(S[f"{k}_rstd"], 1)
                    after(S[f"{k}_rstd"], nth(b, 2, 1))
                    nc.gpsimd.tensor_tensor(rstd[k][:], var[k][:], power[:], ALU.pow).then_inc(S[f"{k}_rstd"], 1)
                return step

            def a_elu_a(b):
                gate(S["e1_ready"], b)
                nc.gpsimd.tensor_scalar(e1m[:], e1[:], 1.0, None, ALU.min).then_inc(S["e1m_ready"], 1)

            def clip(k):
                def step(b):
                    gate(S[f"{k}_ea"], b)
                    nc.gpsimd.tensor_scalar(eb[k][:], ea[k][:], 1.0, None, ALU.min).then_inc(S[f"{k}_eb"], 1)
                return step

            def q_turn(b):
                after(S["q_xn"], b)
                nc.gpsimd.tensor_tensor(xs[:], x1[:], xn["q"][:], ALU.add).then_inc(S["xs_ready"], 1)

            def q_gelu_b(b):
                gate(S["gsq_ready"], b)
                nc.gpsimd.tensor_scalar(gpl[:], gsq[:], GELU_CUBE, 1.0, ALU.mult, ALU.add).then_inc(S["gpl_ready"], 1)

            def m_turn(b):
                if not (isinstance(b, int) and b < 2):
                    gate(S["x4_ready"], b - 1)
                after(S["m_xn"], b)
                nc.gpsimd.tensor_tensor(x3b[:], x3[:], c_lin[:, None, :].to_broadcast([P, U, D]),
                                        ALU.add).then_inc(S["x3b_ready"], 1)

            def m_dt(b):
                after(S["dt_copied"], b)
                nc.gpsimd.tensor_tensor(dt_a[:], dt_raw[:], c_dt[:, :, :].rearrange("p u h -> p (u h)"),
                                        ALU.add).then_inc(S["dt_a_ready"], 1)

            CHAIN = 13

            def m_dt_log(b):
                gate(S["dt_e_ready"], b)
                w = dt_w
                links = [
                    lambda: nc.gpsimd.tensor_tensor(w[0][:], dt_e[:], twos[:], ALU.add),
                    lambda: nc.gpsimd.tensor_tensor(w[1][:], w[0][:], inverse[:], ALU.pow),
                    lambda: nc.gpsimd.tensor_tensor(w[2][:], dt_e[:], w[1][:], ALU.mult),
                    lambda: nc.gpsimd.tensor_tensor(w[3][:], w[2][:], w[2][:], ALU.mult),
                    lambda: nc.gpsimd.tensor_tensor(w[4][:], log_c[:, 4, :], w[3][:], ALU.mult),
                    lambda: nc.gpsimd.tensor_tensor(w[5][:], w[4][:], log_c[:, 3, :], ALU.add),
                    lambda: nc.gpsimd.tensor_tensor(w[6][:], w[5][:], w[3][:], ALU.mult),
                    lambda: nc.gpsimd.tensor_tensor(w[7][:], w[6][:], log_c[:, 2, :], ALU.add),
                    lambda: nc.gpsimd.tensor_tensor(w[8][:], w[7][:], w[3][:], ALU.mult),
                    lambda: nc.gpsimd.tensor_tensor(w[9][:], w[8][:], log_c[:, 1, :], ALU.add),
                    lambda: nc.gpsimd.tensor_tensor(w[10][:], w[9][:], w[3][:], ALU.mult),
                    lambda: nc.gpsimd.tensor_tensor(w[11][:], w[10][:], log_c[:, 0, :], ALU.add),
                    lambda: nc.gpsimd.tensor_tensor(w[12][:], w[11][:], w[2][:], ALU.mult),
                ]
                assert len(links) == CHAIN
                for i, link in enumerate(links):
                    if i:
                        pool.wait_ge(S["dt_chain"], nth(b, CHAIN, i))
                    link().then_inc(S["dt_chain"], 1)
                after(S["dt_chain"], b * CHAIN)
                nc.gpsimd.tensor_tensor(dt[:, :, :].rearrange("p u h -> p (u h)"), w[12][:], dt_p[:],
                                        ALU.add).then_inc(S["dt_ready"], 1)

            def m_da(b):
                after(S["dt_ready"], b)
                nc.gpsimd.tensor_tensor(dA[:], dt[:], a_row[:], ALU.mult)
                nc.gpsimd.tensor_scalar(dt8[:], dt[:], 0.125, None, ALU.mult).then_inc(S["da_ready"], 1)

            def m_conv_a(b):
                for c, i in ((4, 1), (0, 2), (2, 3)):
                    gate(S["xbc_ready"], nth(b, 3, i), i)
                    for k in range(c, min(c + 2, KX)):
                        last = nc.gpsimd.tensor_scalar(acc[:, k, :], xbc[:, k, PAD:PAD + N],
                                                       w_conv[:, k, PAD:PAD + 1], c_conv[:, k:k + 1],
                                                       ALU.mult, ALU.add)
                last.then_inc(S["acc_ready"], 1)

            def m_rms(b):
                gate(S["ss_ready"], b)
                nc.gpsimd.tensor_scalar(ms[:], ss[:], 1.0 / DI, 4.0 * EPS, ALU.mult, ALU.add)\
                    .then_inc(S["rms_ready"], 1)
                after(S["rms_ready"], nth(b, 2, 1))
                nc.gpsimd.tensor_tensor(rms[:], ms[:], power[:], ALU.pow).then_inc(S["rms_ready"], 1)

            turns(nc.gpsimd, dict(
                a_norm=rstd_of("a"), q_norm=rstd_of("q"), g_norm=rstd_of("g"), m_norm=rstd_of("m"),
                a_elu_a=a_elu_a, b_elu_a=clip("b"), g_elu_a=clip("g"), q_turn=q_turn, q_gelu_b=q_gelu_b,
                m_turn=m_turn, m_dt=m_dt, m_dt_log=m_dt_log, m_da=m_da, m_conv_a=m_conv_a, m_rms=m_rms))

        @block.scalar
        def _(act):
            def evac_T(k, src):
                def step(b):
                    act.wait_ge(S[f"{k}_xT_ps"], b)
                    nc.scalar.copy(xT[k][:], two(src)).then_inc(S[f"{k}_xT"], 1)
                return step

            def a_mlp1(b):
                for ps, i, m0 in ((A1, 1, 0), (A2, 2, 2)):
                    act.wait_ge(S["o1_ps"], nth(b, 2, i))
                    for m in (m0, m0 + 1):
                        last = nc.scalar.activation(o1T[:, m, :], ps[:, (m - m0) * N:(m - m0 + 1) * N], ACT.Relu,
                                                    bias=c_mlp1[:, m:m + 1])
                last.then_inc(S["o1_ready"], 1)

            def a_fc(b):
                act.wait_ge(S["h1_ps"], nth(b, 2, 1))
                nc.scalar.activation(h1[:, 0, :], A0[:, :], ACT.Identity, bias=1.0).then_inc(S["h1_a"], 1)

            def a_factors(b):
                act.wait_ge(S["gcol_ready"], b)
                nc.scalar.activation(bcol[:], gcol[:], ACT.Exp)
                nc.scalar.activation(dcol[:], gcol[:], ACT.Exp, scale=ALPHA).then_inc(S["bd_ready"], 1)
                act.wait_ge(S["args_ready"], b)
                nc.scalar.activation(fac[:], args[:], ACT.Exp).then_inc(S["fac_ready"], 1)
                act.wait_ge(S["fac_ready"], b)
                act.wait_ge(S["bd_ready"], b)
                for u in range(U):
                    last = nc.scalar.activation(low[:, u, :], fac[:, 1, :], ACT.Copy, scale=dcol[:, u:u + 1])
                last.then_inc(S["low_ready"], 1)

            def a_att(b):
                act.wait_ge(S["y1_ps"], b)
                act.wait_ge(S["r1_ready"], b)
                for u in range(U):
                    last = nc.scalar.activation(e1[:, u, :], (A0, A1)[u][:, :], ACT.Exp, bias=-1.0,
                                                scale=r1[:, u:u + 1])
                last.then_inc(S["e1_ready"], 1)

            def a_elu_b(b):
                act.wait_ge(S["e1m_ready"], b)
                nc.scalar.activation(e1x[:], e1m[:], ACT.Exp, bias=-1.0).then_inc(S["e1x_ready"], 1)

            def a_mlp2(b):
                act.wait_ge(S["o2_ps"], b)
                for m in range(KD):
                    last = nc.scalar.activation(o2T[:, m, :], A1[:, m * N:(m + 1) * N], ACT.Relu,
                                                bias=c_mlp2[:, m:m + 1])
                last.then_inc(S["o2_ready"], 1)

            def proj(k, ps):
                def step(b):
                    act.wait_ge(S[f"{k}_h_ps"], b)
                    nc.scalar.activation(hp[k][:], two(ps), ACT.Identity, bias=1.0).then_inc(S[f"{k}_hp"], 1)
                return step

            def softmax(k):
                def step(b):
                    act.wait_ge(S[f"{k}_nmax"], b)
                    for u in range(U):
                        last = nc.scalar.activation(pr[k][:, u, :], lr[k][:, u, :], ACT.Exp,
                                                    bias=nmax[k][:, u:u + 1], accum_out=rs[k][:, u:u + 1])
                    last.then_inc(S[f"{k}_pr"], 1)
                return step

            def pturn(k, ps):
                def step(b):
                    act.wait_ge(S[f"{k}_pT_ps"], b)
                    nc.scalar.copy(pT[k][:], two(ps)).then_inc(S[f"{k}_pT"], 1)
                return step

            def elu_exp(k, ps):
                def step(b):
                    act.wait_ge(S[f"{k}_y_ps"], b)
                    act.wait_ge(S[f"{k}_rr"], b)
                    for u in range(U):
                        last = nc.scalar.activation(ea[k][:, u, :], two(ps)[:, u, :], ACT.Exp, bias=-1.0,
                                                    scale=rr[k][:, u:u + 1])
                    last.then_inc(S[f"{k}_ea"], 1)
                return step

            def b_elu_b(b):
                act.wait_ge(S["b_eb"], b)
                nc.scalar.activation(ec[:], eb["b"][:], ACT.Exp, bias=-1.0).then_inc(S["b_ec"], 1)

            def q_route(b):
                act.wait_ge(S["w_ps"], b)
                nc.scalar.activation(wrow[:], Q1[:, 0:N], ACT.Identity, bias=c_route[:, 0:1])\
                    .then_inc(S["wrow_ready"], 1)

            def q_select(b):
                act.wait_ge(S["pickT_ps"], b)
                nc.scalar.copy(pickT[:], Q1[:, 0:N]).then_inc(S["pickT_ready"], 1)

            def q_gather(b):
                act.wait_ge(S["sel_ps"], b)
                nc.scalar.copy(selT[:], Q0[:, 0:KD * P].rearrange("p (k r) -> p k r", k=KD))\
                    .then_inc(S["sel_ready"], 1)

            def q_gelu_a(b):
                act.wait_ge(S["ga_ready"], b)
                nc.scalar.activation(gsq[:], ga_[:], ACT.Square).then_inc(S["gsq_ready"], 1)

            def q_gelu_c(b):
                act.wait_ge(S["gq_ready"], b)
                nc.scalar.activation(gt[:], gq[:], ACT.Tanh, scale=GELU_SCALE).then_inc(S["gt_ready"], 1)

            def m_xbc_a(b):
                act.wait_ge(S["xbc_ps"], nth(b, 3, 1))
                nc.scalar.copy(dt_raw[:], M1[:, 0:U * NH]).then_inc(S["dt_copied"], 1)
                nc.scalar.copy(xbc[:, 4, PAD:], M1[:, N:2 * N]).then_inc(S["xbc_ready"], 1)
                act.wait_ge(S["xbc_ps"], nth(b, 3, 2))
                nc.scalar.copy(xbc[:, 0:2, PAD:], two(M2)).then_inc(S["xbc_ready"], 1)

            def m_xbc_b(b):
                act.wait_ge(S["xbc_ps"], nth(b, 3, 3))
                nc.scalar.copy(xbc[:, 2:4, PAD:], two(M0)).then_inc(S["xbc_ready"], 1)

            def m_dt_exp(b):
                act.wait_ge(S["dt_a_ready"], b)
                nc.scalar.activation(dt_w[13][:], dt_a[:], ACT.Abs).then_inc(S["dt_abs"], 1)
                act.wait_ge(S["dt_abs"], b)
                nc.scalar.activation(dt_p[:], dt_a[:], ACT.Relu)
                nc.scalar.activation(dt_e[:], dt_w[13][:], ACT.Exp, scale=-1.0).then_inc(S["dt_e_ready"], 1)

            def m_silu(b):
                act.wait_ge(S["conv"], nth(b, 3, 3))
                before(act, S["ss_ready"], b)
                nc.scalar.activation(th[:], acc[:], ACT.Tanh, scale=0.5).then_inc(S["th_ready"], 1)

            def m_z(b):
                for u in range(U):
                    act.wait_ge(S["z_ps"], nth(b, 2, u + 1))
                    nc.scalar.activation(tz[:, u, :], (M2, M0)[u][:, :], ACT.Tanh, scale=0.5)\
                        .then_inc(S["tz_ready"], 1)

            def m_decay(b):
                act.wait_ge(S["decarg_ready"], b)
                nc.scalar.activation(dec0[:], dec0[:], ACT.Exp)
                nc.scalar.activation(dec1[:], dec1[:], ACT.Exp).then_inc(S["dec_ready"], 1)

            def m_gated(b):
                for u in range(U):
                    act.wait_ge(S["yg_ready"], nth(b, 2, u + 1))
                    last = nc.scalar.activation(ysq[:, u, :], yg[:, u, :], ACT.Square, accum_out=ss[:, u:u + 1])
                last.then_inc(S["ss_ready"], 1)

            def m_yturn(b):
                for i, ps in ((1, M0), (2, M1)):
                    act.wait_ge(S["yT_ps"], nth(b, 2, i))
                    last = nc.scalar.copy(ygT[:, 2 * i - 2:2 * i, :], two(ps))
                last.then_inc(S["yT_ready"], 1)

            turns(nc.scalar, dict(
                a_turn=evac_T("a", A0), q_turn=evac_T("q", Q0), g_turn=evac_T("g", Q0), m_turn=evac_T("m", M0),
                a_mlp1=a_mlp1, a_fc=a_fc, a_factors=a_factors, a_att=a_att, a_elu_b=a_elu_b, a_mlp2=a_mlp2,
                b_proj=proj("b", A2), g_proj=proj("g", Q1),
                b_exp=softmax("b"), g_exp=softmax("g"), b_pturn=pturn("b", A0), g_pturn=pturn("g", Q0),
                b_att=elu_exp("b", A2), g_att=elu_exp("g", Q1), b_elu_b=b_elu_b,
                q_route=q_route, q_select=q_select, q_gather=q_gather, q_gelu_a=q_gelu_a, q_gelu_c=q_gelu_c,
                m_xbc_a=m_xbc_a, m_xbc_b=m_xbc_b, m_dt_exp=m_dt_exp, m_silu=m_silu, m_z=m_z, m_decay=m_decay,
                m_gated=m_gated, m_yturn=m_yturn))

        @block.vector
        def _(v):
            def stats(k, src, ready):
                def step(b):
                    v.wait_ge(*((x_loaded, 16 * b) if ready is None else (S[ready], b)))
                    for u in range(U):
                        last = nc.vector.bn_stats(bn[k][:, u, :], src[:, u, :])
                    last.then_inc(S[f"{k}_stats"], 1)
                    v.wait_ge(S[f"{k}_stats"], nth(b, 2, 1))
                    nc.vector.memset(hold_cols[:, "aqgm".index(k):"aqgm".index(k) + 1], 0.0)
                    for u in range(U):
                        last = nc.vector.bn_aggr(mv[k][:, u, :], bn[k][:, u, :])
                    last.then_inc(S[f"{k}_stats"], 1)
                return step

            def norm(k, src):
                def step(b):
                    v.wait_ge(S[f"{k}_rstd"], nth(b, 2, 2))
                    for u in range(U):
                        last = nc.vector.tensor_scalar(xn[k][:, u, :], src[:, u, :], mv[k][:, u, 0:1],
                                                       rstd[k][:, u:u + 1], ALU.subtract, ALU.mult)
                    last.then_inc(S[f"{k}_xn"], 1)
                return step

            def a_fc(b):
                v.wait_ge(S["h1_ps"], nth(b, 2, 2))
                nc.vector.tensor_scalar(h1[:, 1, :], A1[:, :], 1.0, None, ALU.add).then_inc(S["h1_b"], 1)

            def a_fcol(b):
                v.wait_ge(S["f1_ps"], b)
                nc.vector.tensor_copy(f1[:, :, :].rearrange("p u k -> p (u k)"), A2[:, 0:2 * U])\
                    .then_inc(S["f1_ready"], 1)

            def a_maxima(b):
                v.wait_ge(S["fb_ps"], b)
                nc.vector.tensor_reduce(top[:], A2[:, N:2 * N], AX_X, ALU.max).then_inc(S["top_ready"], 1)
                v.wait_ge(S["top_ready"], b)
                nc.vector.tensor_scalar(arg[:], A2[:, 0:N], top[:, 0:1], 1.0 - ALPHA, ALU.add, ALU.mult)\
                    .then_inc(S["arg_ready"], 1)
                nc.vector.tensor_scalar(gcol[:], f1[:, :, 1], top[:, 0:1], None, ALU.subtract)\
                    .then_inc(S["gcol_ready"], 1)
                v.wait_ge(S["arg_ready"], b)
                nc.vector.tensor_scalar(args[:, 0, :], arg[:], 0.0, None, ALU.min)
                nc.vector.tensor_scalar(args[:, 1, :], arg[:], 0.0, -1.0, ALU.max, ALU.mult)\
                    .then_inc(S["args_ready"], 1)

            def a_probs(b):
                v.wait_ge(S["low_ready"], b)
                for u in range(U):
                    last = nc.vector.scalar_tensor_tensor(out=p1[:, u, :], in0=fac[:, 0, :], scalar=bcol[:, u:u + 1],
                                                          in1=low[:, u, :], op0=ALU.mult, op1=ALU.max)
                last.then_inc(S["p1_ready"], 1)

            def a_att(b):
                v.wait_ge(S["s1_ps"], b)
                nc.vector.reciprocal(r1[:], A2[:, 0:U]).then_inc(S["r1_ready"], 1)

            def a_elu_c(b):
                v.wait_ge(S["e1x_ready"], b)
                for u in range(U):
                    last = nc.vector.scalar_tensor_tensor(out=u1[:, u, :], in0=(A0, A1)[u][:, :], scalar=r1[:, u:u + 1],
                                                          in1=e1x[:, u, :], op0=ALU.mult, op1=ALU.max)
                last.then_inc(S["u1_ready"], 1)

            def a_uturn(b):
                for i, ps, c in ((1, A2, 0), (2, A0, 2)):
                    v.wait_ge(S["u1T_ps"], nth(b, 2, i))
                    last = nc.vector.scalar_tensor_tensor(out=z1T[:, c:c + 2, :].rearrange("p c n -> p (c n)"), in0=ps[:, :],
                                                   scalar=-1.0, in1=o1T[:, c:c + 2, :].rearrange("p c n -> p (c n)"),
                                                          op0=ALU.add, op1=ALU.add)
                last.then_inc(S["z1_ready"], 1)

            def fcol(k, ps):
                def step(b):
                    v.wait_ge(S[f"{k}_f_ps"], b)
                    nc.vector.tensor_copy(fc[k][:, :, :].rearrange("p u k -> p (u k)"), ps[:, 0:2 * U])\
                        .then_inc(S[f"{k}_fc"], 1)
                return step

            def mask(k, ps, m):
                def step(b):
                    v.wait_ge(S[f"{k}_fb_ps"], b)
                    for u in range(U):
                        last = nc.vector.scalar_tensor_tensor(out=sc[k][:, u, :], in0=m[:, u, :],
                                                              scalar=fc[k][:, u, 0:1], in1=ps[:, N:2 * N],
                                                              op0=ALU.add, op1=ALU.add)
                    last.then_inc(S[f"{k}_sc"], 1)
                return step

            def lrelu(k):
                def step(b):
                    v.wait_ge(S[f"{k}_sc"], b)
                    nc.vector.scalar_tensor_tensor(out=lr[k][:], in0=sc[k][:], scalar=ALPHA, in1=sc[k][:],
                                                   op0=ALU.mult, op1=ALU.max).then_inc(S[f"{k}_lr"], 1)
                return step

            def rowmax(k):
                def step(b):
                    v.wait_ge(S[f"{k}_lr"], b)
                    nc.vector.tensor_reduce(nmax[k][:], lr[k][:], AX_X, ALU.max, negate=True)\
                        .then_inc(S[f"{k}_nmax"], 1)
                return step

            def rowsum(k):
                def step(b):
                    v.wait_ge(S[f"{k}_pr"], b)
                    nc.vector.reciprocal(rr[k][:], rs[k][:]).then_inc(S[f"{k}_rr"], 1)
                return step

            def elu_max(k, ps, e, ready):
                def step(b):
                    v.wait_ge(S[ready], b)
                    for u in range(U):
                        last = nc.vector.scalar_tensor_tensor(out=ue[k][:, u, :], in0=two(ps)[:, u, :],
                                                              scalar=rr[k][:, u:u + 1], in1=e[:, u, :],
                                                              op0=ALU.mult, op1=ALU.max)
                    last.then_inc(S[f"{k}_ue"], 1)
                return step

            def b_x1(b):
                v.wait_ge(S["b_ue"], b)
                v.wait_ge(S["res_ps"], b)
                nc.vector.scalar_tensor_tensor(out=v1[:, :, :].rearrange("p u d -> p (u d)"), in0=A1[:, :], scalar=-1.0,
                                               in1=ue["b"][:, :, :].rearrange("p u d -> p (u d)"), op0=ALU.add,
                                               op1=ALU.add).then_inc(S["v1_ready"], 1)
                v.wait_ge(S["v1_ready"], b)
                v.wait_ge(x0_loaded, 16 * b)
                before(v, S["xs_ready"], b)
                nc.vector.scalar_tensor_tensor(out=x1[:], in0=v1[:], scalar=0.0, in1=x0[:], op0=ALU.max, op1=ALU.add)\
                    .then_inc(S["x1_ready"], 1)

            def g_x3(b):
                v.wait_ge(S["g_ue"], b)
                before(v, S["x3b_ready"], b)
                nc.vector.scalar_tensor_tensor(out=x3[:], in0=ue["g"][:], scalar=-1.0, in1=x2[:], op0=ALU.add,
                                               op1=ALU.add).then_inc(S["x3_ready"], 1)

            def q_route_col(b):
                v.wait_ge(S["wrow_ready"], b)
                for u in range(U):
                    last = nc.vector.scalar_tensor_tensor(out=junk[:, u * P:(u + 1) * P], in0=wrow[:, u * P:(u + 1) * P],
                                                          scalar=1.0, in1=ident[:], op0=ALU.mult, op1=ALU.mult,
                                                          accum_out=wcol[:, u:u + 1])
                last.then_inc(S["wcol_ready"], 1)

            def q_rank(b):
                v.wait_ge(S["wcol_ready"], b)
                spare = gsq[:, :, :].rearrange("p (a c) r -> p a (c r)", a=4)
                for u in range(U):
                    nc.vector.tensor_scalar(spare[:, 2 * u, :], wrow[:], wcol[:, u:u + 1], None,
                                            ALU.is_gt, ALU.add, accum_out=above[:, u:u + 1])
                    last = nc.vector.scalar_tensor_tensor(out=spare[:, 2 * u + 1, :], in0=wrow[:],
                                                          scalar=wcol[:, u:u + 1], in1=earlier[:, u, :],
                                                          op0=ALU.is_equal, op1=ALU.mult,
                                                          accum_out=ties[:, u:u + 1])
                last.then_inc(S["counts_ready"], 1)
                v.wait_ge(S["counts_ready"], b)
                nc.vector.tensor_tensor(rank[:], above[:], ties[:], ALU.add).then_inc(S["rank_ready"], 1)
                v.wait_ge(S["rank_ready"], b)
                for u in range(U):
                    last = nc.vector.tensor_scalar(pick[:, u, :], slot[:], rank[:, u:u + 1], None, ALU.is_equal)
                last.then_inc(S["pick_ready"], 1)

            def q_gelu_a(b):
                for i, ps, k in ((1, Q0, 0), (2, Q1, KF // 2)):
                    v.wait_ge(S["up_ps"], nth(b, 2, i))
                    last = nc.vector.tensor_tensor(ga_[:, k:k + KF // 2, :], ps[:, :].rearrange("p (k r) -> p k r", r=P),
                                                   c_up[:, k:k + KF // 2, None].to_broadcast([P, KF // 2, P]), ALU.add)
                last.then_inc(S["ga_ready"], 1)

            def q_gelu_b(b):
                v.wait_ge(S["gpl_ready"], b)
                nc.vector.tensor_tensor(gq[:], gpl[:], ga_[:], ALU.mult).then_inc(S["gq_ready"], 1)

            def q_ffn2(b):
                v.wait_ge(S["gt_ready"], b)
                nc.vector.scalar_tensor_tensor(out=gl[:], in0=gt[:], scalar=1.0, in1=ga_[:], op0=ALU.add, op1=ALU.mult)\
                    .then_inc(S["gl_ready"], 1)

            def q_scatter(b):
                v.wait_ge(S["yff_ps"], b)
                nc.vector.tensor_tensor(yff[:], Q0[:, 0:D], c_down[:], ALU.add).then_inc(S["yff_ready"], 1)

            def q_x2(b):
                v.wait_ge(S["sc_ps"], b)
                v.wait_ge(S["xs_ready"], b)
                for u in range(U):
                    last = nc.vector.scalar_tensor_tensor(out=x2[:, u, :], in0=two(Q1)[:, u, :], scalar=wcol[:, u:u + 1],
                                                          in1=xs[:, u, :], op0=ALU.mult, op1=ALU.add)
                last.then_inc(S["x2_ready"], 1)

            def m_conv_b(b):
                v.wait_ge(S["acc_ready"], b)
                for i in range(PAD):
                    if i:
                        v.wait_ge(S["conv"], nth(b, 3, i))
                    tap = PAD - 1 - i
                    for k in range(KX):
                        last = nc.vector.scalar_tensor_tensor(out=acc[:, k, :], in0=xbc[:, k, tap:tap + N],
                                                              scalar=w_conv[:, k, tap:tap + 1], in1=acc[:, k, :],
                                                              op0=ALU.mult, op1=ALU.add)
                    last.then_inc(S["conv"], 1)

            def m_silu(b):
                v.wait_ge(S["th_ready"], b)
                c = acc
                nc.vector.scalar_tensor_tensor(out=xc[:, 0:KI, :], in0=th[:, 0:KI, :], scalar=1.0, in1=c[:, 0:KI, :],
                                               op0=ALU.add, op1=ALU.mult)
                nc.vector.scalar_tensor_tensor(out=bT[:], in0=th[0:DS, KI, :], scalar=1.0, in1=c[0:DS, KI, :],
                                               op0=ALU.add, op1=ALU.mult)
                nc.vector.scalar_tensor_tensor(out=cT[:], in0=th[DS:, KI, :], scalar=1.0, in1=c[DS:, KI, :],
                                               op0=ALU.add, op1=ALU.mult).then_inc(S["xc_ready"], 1)

            def m_scan(b):
                v.wait_ge(S["dA_ps"], b)
                nc.vector.tensor_tensor_scan(cumT[0:NH, :], ones[0:NH, :], M1[0:NH, 0:N], 0.0, ALU.mult, ALU.add)\
                    .then_inc(S["cumT_ready"], 1)

            def m_cum_col(b):
                v.wait_ge(S["cumc_ps"], b)
                nc.vector.tensor_copy(cumcol[:], M1[:, 0:U * P].rearrange("p (u h) -> p u h", u=U)[:, :, 0:NH])\
                    .then_inc(S["cumcol_ready"], 1)

            def m_cb(b):
                v.wait_ge(S["cb_ps"], b)
                nc.vector.tensor_tensor(cb[:], M1[:, 0:N + P], causal[:], ALU.mult).then_inc(S["cb_ready"], 1)

            def m_gate(b):
                for u in range(U):
                    v.wait_ge(S["tz_ready"], nth(b, 2, u + 1))
                    nc.vector.scalar_tensor_tensor(out=gz[:, u, :], in0=tz[:, u, :], scalar=1.0, in1=(M2, M0)[u][:, :],
                                                   op0=ALU.add, op1=ALU.mult).then_inc(S["gz_ready"], 1)

            def m_xrow(b):
                for u in range(U):
                    v.wait_ge(S["xr_ps"], nth(b, 2, u + 1))
                    nc.vector.tensor_tensor(xdt[:, u, :].rearrange("p (h d) -> p h d", h=NH),
                                            (M2, M0)[u][:, :].rearrange("p (h d) -> p h d", h=NH),
                                            dt8[:, u, :, None].to_broadcast([P, NH, HD]), ALU.mult)\
                        .then_inc(S["xdt_ready"], 1)

            def m_mix(b):
                v.wait_ge(S["dec_ready"], b)
                v.wait_ge(S["cb_ready"], b)
                nc.vector.tensor_tensor(dec0[:], dec0[:], cb[:, None, 0:N].to_broadcast([P, NH, N]), ALU.mult)
                nc.vector.tensor_tensor(dec1[:], dec1[:], cb[:, None, N:].to_broadcast([P, NH, P]), ALU.mult)\
                    .then_inc(S["mix_ready"], 1)

            def m_decay(b):
                v.wait_ge(S["cumcol_ready"], b)
                v.wait_ge(cum_spread, 16 * b)
                for h in range(NH):
                    nc.vector.tensor_scalar(dec0[:, h, :], cumB[:, h, :], cumcol[:, 0, h:h + 1], 0.0,
                                            ALU.subtract, ALU.min)
                    last = nc.vector.tensor_scalar(dec1[:, h, :], cumB[:, h, P:], cumcol[:, 1, h:h + 1], 0.0,
                                                   ALU.subtract, ALU.min)
                last.then_inc(S["decarg_ready"], 1)

            def m_y(b):
                for u in range(U):
                    v.wait_ge(S["y_ps"], nth(b, 2, u + 1))
                    nc.vector.tensor_tensor(yg[:, u, :], (M1, M2)[u][:, :], gz[:, u, :], ALU.mult)\
                        .then_inc(S["yg_ready"], 1)

            def m_out(b):
                v.wait_ge(S["out_ps"], b)
                v.wait_ge(S["rms_ready"], nth(b, 2, 2))
                v.wait_ge(S["x3b_ready"], b)
                if not (isinstance(b, int) and b < 2):
                    v.wait_ge(out_stored, 16 * (b - 1))
                for u in range(U):
                    last = nc.vector.scalar_tensor_tensor(out=x4[:, u, :], in0=two(M2)[:, u, :], scalar=rms[:, u:u + 1],
                                                          in1=x3b[:, u, :], op0=ALU.mult, op1=ALU.add)
                last.then_inc(S["x4_ready"], 1)

            turns(nc.vector, dict(
                a_stats=stats("a", x_in, None), q_stats=stats("q", x1, "x1_ready"),
                g_stats=stats("g", x2, "x2_ready"), m_stats=stats("m", x3, "x3_ready"),
                a_norm=norm("a", x_in), q_norm=norm("q", x1), g_norm=norm("g", x2), m_norm=norm("m", x3),
                a_fc=a_fc, a_fcol=a_fcol, a_maxima=a_maxima, a_probs=a_probs, a_att=a_att, a_elu_c=a_elu_c,
                a_uturn=a_uturn, b_proj=fcol("b", A0), g_proj=fcol("g", Q0), b_mask=mask("b", A0, mask0),
                g_mask=mask("g", Q0, mask1), b_lrelu=lrelu("b"), g_lrelu=lrelu("g"), b_max=rowmax("b"), g_max=rowmax("g"), b_pturn=rowsum("b"),
                g_pturn=rowsum("g"), b_elu_c=elu_max("b", A2, ec, "b_ec"), g_elu_b=elu_max("g", Q1, eb["g"], "g_eb"),
                b_x1=b_x1, g_x3=g_x3, q_route_col=q_route_col, q_rank=q_rank, q_gelu_a=q_gelu_a, q_gelu_b=q_gelu_b,
                q_ffn2=q_ffn2, q_scatter=q_scatter, q_x2=q_x2, m_conv_b=m_conv_b, m_silu=m_silu, m_scan=m_scan,
                m_cum_col=m_cum_col, m_cb=m_cb, m_gate=m_gate, m_xrow=m_xrow, m_decay=m_decay, m_mix=m_mix, m_y=m_y, m_out=m_out))

        @block.tensor
        def _(pe):
            def turn_rows(k, ps, freed=None):
                def step(b):
                    pe.wait_ge(S[f"{k}_xn"], b)
                    if freed is not None:
                        before(pe, S[freed], b)
                    for c in range(KD):
                        for u in range(U):
                            last = nc.tensor.transpose(ps[:, c * N + u * P:c * N + (u + 1) * P],
                                                       xn[k][:, u, c * P:(c + 1) * P], ident[:])
                    last.then_inc(S[f"{k}_xT_ps"], 1)
                return step

            def a_mlp1(b):
                pe.wait_ge(S["a_xT"], b)
                before(pe, S["v1_ready"], b)
                for ps, m0 in ((A1, 0), (A2, 2)):
                    for m in (m0, m0 + 1):
                        for k in range(KD):
                            last = nc.tensor.matmul(ps[:, (m - m0) * N:(m - m0 + 1) * N],
                                                    w_mlp1[:, k, m * P:(m + 1) * P], xT["a"][:, k, :],
                                                    start=(k == 0), stop=(k == KD - 1))
                    last.then_inc(S["o1_ps"], 1)

            def a_fc(b):
                pe.wait_ge(S["o1_ready"], b)
                for u in range(U):
                    for k in range(KH):
                        last = nc.tensor.matmul((A0, A1)[u][:, :], o1T[:, k, u * P:(u + 1) * P], w_fc[:, k, :],
                                                start=(k == 0), stop=(k == KH - 1))
                    last.then_inc(S["h1_ps"], 1)
                for u in range(U):
                    for k in range(KH):
                        last = nc.tensor.matmul(A2[:, 2 * u:2 * u + 2], o1T[:, k, u * P:(u + 1) * P], v_fc[:, k, :],
                                                start=(k == 0), stop=(k == KH - 1))
                last.then_inc(S["f1_ps"], 1)

            def a_bcast(b):
                pe.wait_ge(S["f1_ready"], b)
                for half in range(2):
                    for u in range(U):
                        last = nc.tensor.matmul(A2[:, half * N + u * P:half * N + (u + 1) * P],
                                                f1[:, u, half:half + 1].to_broadcast([P, P]), ident[:],
                                                start=True, stop=True)
                last.then_inc(S["fb_ps"], 1)

            def a_att(b):
                pe.wait_ge(S["p1_ready"], b)
                for u in range(U):
                    for j in range(U):
                        last = nc.tensor.matmul(A2[:, u:u + 1], p1[:, j, u * P:(u + 1) * P], ones[:, 0:1],
                                                start=(j == 0), stop=(j == U - 1))
                last.then_inc(S["s1_ps"], 1)
                pe.wait_ge(S["h1_a"], b)
                pe.wait_ge(S["h1_b"], b)
                for u in range(U):
                    for j in range(U):
                        last = nc.tensor.matmul((A0, A1)[u][:, :], p1[:, j, u * P:(u + 1) * P], h1[:, j, :],
                                                start=(j == 0), stop=(j == U - 1))
                last.then_inc(S["y1_ps"], 1)

            def a_uturn(b):
                pe.wait_ge(S["u1_ready"], b)
                for ps, c0 in ((A2, 0), (A0, 2)):
                    for c in (c0, c0 + 1):
                        for u in range(U):
                            last = nc.tensor.transpose(ps[:, (c - c0) * N + u * P:(c - c0) * N + (u + 1) * P],
                                                       u1[:, u, c * P:(c + 1) * P], ident[:])
                    last.then_inc(S["u1T_ps"], 1)

            def a_mlp2(b):
                pe.wait_ge(S["z1_ready"], b)
                for m in range(KD):
                    for k in range(KH):
                        last = nc.tensor.matmul(A1[:, m * N:(m + 1) * N], w_mlp2[:, k, m * P:(m + 1) * P],
                                                z1T[:, k, :], start=(k == 0), stop=(k == KH - 1))
                last.then_inc(S["o2_ps"], 1)

            def proj(k, ready, src, w, vec, ps_f, ps_h):
                def step(b):
                    pe.wait_ge(S[ready], b)
                    for u in range(U):
                        for c in range(KD):
                            last = nc.tensor.matmul(ps_f[:, 2 * u:2 * u + 2], src[:, c, u * P:(u + 1) * P], vec[:, c, :],
                                                    start=(c == 0), stop=(c == KD - 1))
                    last.then_inc(S[f"{k}_f_ps"], 1)
                    for u in range(U):
                        for c in range(KD):
                            last = nc.tensor.matmul(ps_h[:, u * D:(u + 1) * D], src[:, c, u * P:(u + 1) * P], w[:, c, :],
                                                    start=(c == 0), stop=(c == KD - 1))
                    last.then_inc(S[f"{k}_h_ps"], 1)
                return step

            def bcast(k, ps):
                def step(b):
                    pe.wait_ge(S[f"{k}_fc"], b)
                    for u in range(U):
                        last = nc.tensor.matmul(ps[:, N + u * P:N + (u + 1) * P],
                                                fc[k][:, u, 1:2].to_broadcast([P, P]), ident[:], start=True, stop=True)
                    last.then_inc(S[f"{k}_fb_ps"], 1)
                    if k == "b":
                        for u in range(U):
                            for c in range(KD):
                                last = nc.tensor.transpose(A1[:, u * D + c * P:u * D + (c + 1) * P],
                                                           o2T[:, c, u * P:(u + 1) * P], ident[:])
                        last.then_inc(S["res_ps"], 1)
                return step

            def pturn(k, ps):
                def step(b):
                    pe.wait_ge(S[f"{k}_pr"], b)
                    for j in range(U):
                        for u in range(U):
                            last = nc.tensor.transpose(ps[:, j * N + u * P:j * N + (u + 1) * P],
                                                       pr[k][:, u, j * P:(j + 1) * P], ident[:])
                    last.then_inc(S[f"{k}_pT_ps"], 1)
                return step

            def att(k, ps):
                def step(b):
                    pe.wait_ge(S[f"{k}_pT"], b)
                    pe.wait_ge(S[f"{k}_hp"], b)
                    for u in range(U):
                        for j in range(U):
                            last = nc.tensor.matmul(ps[:, u * D:(u + 1) * D], pT[k][:, j, u * P:(u + 1) * P],
                                                    hp[k][:, j, :], start=(j == 0), stop=(j == U - 1))
                    last.then_inc(S[f"{k}_y_ps"], 1)
                return step

            def q_route(b):
                pe.wait_ge(S["q_xT"], b)
                before(pe, S["g_ue"], b)
                for c in range(KD):
                    last = nc.tensor.matmul(Q1[:, 0:N], w_route_b[:, c, :], xT["q"][:, c, :],
                                            start=(c == 0), stop=(c == KD - 1))
                last.then_inc(S["w_ps"], 1)

            def q_select(b):
                pe.wait_ge(S["pick_ready"], b)
                for u in range(U):
                    last = nc.tensor.transpose(Q1[:, u * P:(u + 1) * P], pick[:, u, :], ident[:])
                last.then_inc(S["pickT_ps"], 1)

            def q_gather(b):
                for c in range(KD):
                    for u in range(U):
                        last = nc.tensor.matmul(Q0[:, c * P:(c + 1) * P], xn["q"][:, u, c * P:(c + 1) * P],
                                                pick[:, u, :], start=(u == 0), stop=(u == U - 1))
                last.then_inc(S["sel_ps"], 1)

            def q_ffn1(b):
                pe.wait_ge(S["sel_ready"], b)
                pe.wait_ge(S["pickT_ready"], b)
                for ps, m0 in ((Q0, 0), (Q1, KF // 2)):
                    for m in range(m0, m0 + KF // 2):
                        for c in range(KD):
                            last = nc.tensor.matmul(ps[:, (m - m0) * P:(m - m0 + 1) * P], w_up[:, c, m * P:(m + 1) * P],
                                                    selT[:, c, :], start=(c == 0), stop=(c == KD - 1))
                    last.then_inc(S["up_ps"], 1)

            def q_ffn2(b):
                pe.wait_ge(S["gl_ready"], b)
                for m in range(KF):
                    last = nc.tensor.matmul(Q0[:, 0:D], gl[:, m, :], w_down[:, m, :], start=(m == 0), stop=(m == KF - 1))
                last.then_inc(S["yff_ps"], 1)

            def q_scatter(b):
                pe.wait_ge(S["yff_ready"], b)
                for u in range(U):
                    last = nc.tensor.matmul(Q1[:, u * D:(u + 1) * D], pickT[:, u * P:(u + 1) * P], yff[:],
                                            start=True, stop=True)
                last.then_inc(S["sc_ps"], 1)

            def xbc_tile(ps, at, k):
                for c in range(KD):
                    last = nc.tensor.matmul(ps[:, at:at + N], w_in[:, c, X0 + k * P:X0 + (k + 1) * P], xT["m"][:, c, :],
                                            start=(c == 0), stop=(c == KD - 1))
                return last

            def m_xbc_a(b):
                pe.wait_ge(S["m_xT"], b)
                for u in range(U):
                    for c in range(KD):
                        nc.tensor.matmul(M1[:, u * NH:(u + 1) * NH], xT["m"][:, c, u * P:(u + 1) * P],
                                         w_in[:, c, DT0:DT0 + NH], start=(c == 0), stop=(c == KD - 1))
                xbc_tile(M1, N, 4).then_inc(S["xbc_ps"], 1)
                before(pe, S["x4_ready"], b)
                xbc_tile(M2, 0, 0)
                xbc_tile(M2, N, 1).then_inc(S["xbc_ps"], 1)

            def m_xbc_b(b):
                xbc_tile(M0, 0, 2)
                xbc_tile(M0, N, 3).then_inc(S["xbc_ps"], 1)

            def m_z(b):
                for u in range(U):
                    pe.wait_ge(S["xbc_ready"], nth(b, 3, u + 2))
                    for c in range(KD):
                        last = nc.tensor.matmul((M2, M0)[u][:, :], xT["m"][:, c, u * P:(u + 1) * P],
                                                w_in[:, c, Z0:Z0 + DI], start=(c == 0), stop=(c == KD - 1))
                    last.then_inc(S["z_ps"], 1)

            def m_da(b):
                pe.wait_ge(S["da_ready"], b)
                pe.wait_ge(S["xbc_ready"], nth(b, 3, 1))
                for u in range(U):
                    last = nc.tensor.transpose(M1[0:NH, u * P:(u + 1) * P], dA[:, u, :], ident[:])
                last.then_inc(S["dA_ps"], 1)

            def m_cum_col(b):
                pe.wait_ge(S["cumT_ready"], b)
                for u in range(U):
                    last = nc.tensor.transpose(M1[:, u * P:(u + 1) * P], cumT[:, u * P:(u + 1) * P], ident[:])
                last.then_inc(S["cumc_ps"], 1)

            def m_cb(b):
                pe.wait_ge(S["xc_ready"], b)
                pe.wait_ge(S["cumcol_ready"], b)
                nc.tensor.matmul(M1[:, 0:N], bT[:, 0:P], cT[:, :], start=True, stop=True)
                nc.tensor.matmul(M1[:, N:N + P], bT[:, P:], cT[:, P:], start=True, stop=True).then_inc(S["cb_ps"], 1)

            def m_xrow(b):
                for u in range(U):
                    pe.wait_ge(S["gz_ready"], nth(b, 2, u + 1))
                    for c in range(KI):
                        last = nc.tensor.transpose((M2, M0)[u][:, c * P:(c + 1) * P], xc[:, c, u * P:(u + 1) * P],
                                                   ident[:])
                    last.then_inc(S["xr_ps"], 1)

            def m_y(b):
                pe.wait_ge(S["mix_ready"], b)
                for u in range(U):
                    ps = (M1, M2)[u]
                    pe.wait_ge(S["xdt_ready"], nth(b, 2, u + 1))
                    for c in range(KI):
                        nc.tensor.matmul(ps[:, c * P:(c + 1) * P], xc[:, c, u * P:(u + 1) * P], d_diag[:, c, :],
                                         start=(c == 0), stop=False, skip_group_check=True)
                    for h in range(NH):
                        for s in range(u + 1):
                            lhsT = dec0[:, h, u * P:(u + 1) * P] if s == 0 else dec1[:, h, :]
                            last = nc.tensor.matmul(ps[:, h * HD:(h + 1) * HD], lhsT, xdt[:, s, h * HD:(h + 1) * HD],
                                                    start=False, stop=(h == NH - 1 and s == u), skip_group_check=True)
                    last.then_inc(S["y_ps"], 1)

            def m_yturn(b):
                pe.wait_ge(S["yg_ready"], nth(b, 2, 2))
                for ps, c0 in ((M0, 0), (M1, 2)):
                    for c in (c0, c0 + 1):
                        for u in range(U):
                            last = nc.tensor.transpose(ps[:, (c - c0) * N + u * P:(c - c0) * N + (u + 1) * P],
                                                       yg[:, u, c * P:(c + 1) * P], ident[:])
                    last.then_inc(S["yT_ps"], 1)

            def m_out(b):
                pe.wait_ge(S["yT_ready"], b)
                for u in range(U):
                    for c in range(KI):
                        last = nc.tensor.matmul(M2[:, u * D:(u + 1) * D], ygT[:, c, u * P:(u + 1) * P], w_comb[:, c, :],
                                                start=(c == 0), stop=(c == KI - 1))
                last.then_inc(S["out_ps"], 1)

            turns(nc.tensor, dict(
                a_turn=turn_rows("a", A0, "b_pT"), q_turn=turn_rows("q", Q0, "g_pT"), g_turn=turn_rows("g", Q0),
                m_turn=turn_rows("m", M0, "yT_ready"), a_mlp1=a_mlp1, a_fc=a_fc, a_bcast=a_bcast, a_att=a_att, a_uturn=a_uturn,
                a_mlp2=a_mlp2, b_proj=proj("b", "o2_ready", o2T, w_hand, v_hand, A0, A2),
                g_proj=proj("g", "g_xT", xT["g"], w_gat, v_gat, Q0, Q1), b_bcast=bcast("b", A0),
                g_bcast=bcast("g", Q0), b_pturn=pturn("b", A0), g_pturn=pturn("g", Q0), b_att=att("b", A2),
                g_att=att("g", Q1), q_route=q_route, q_select=q_select, q_gather=q_gather, q_ffn1=q_ffn1,
                q_ffn2=q_ffn2, q_scatter=q_scatter, m_xbc_a=m_xbc_a, m_xbc_b=m_xbc_b, m_z=m_z, m_da=m_da,
                m_cum_col=m_cum_col, m_cb=m_cb, m_xrow=m_xrow, m_y=m_y, m_yturn=m_yturn, m_out=m_out))


_INS = ["x", "adj", "L0_gnn_mlp1_w", "L0_gnn_mlp1_b", "L0_gnn_mlp2_w", "L0_gnn_mlp2_b", "L0_gnn_W_fc", "L0_gnn_a_fc",
        "L0_gnn_W_hand", "L0_gnn_a_hand", "L0_ffn_wr", "L0_ffn_br", "L0_ffn_w1", "L0_ffn_b1", "L0_ffn_w2", "L0_ffn_b2",
        "L1_gnn_W", "L1_gnn_a", "L1_ffn_W_in", "L1_ffn_conv_w", "L1_ffn_conv_b", "L1_ffn_dt_bias", "L1_ffn_A_log",
        "L1_ffn_D", "L1_ffn_norm_w", "L1_ffn_W_out", "L1_ffn_W_lin", "L1_ffn_b_lin"]


def kernel(**inputs):
    import numpy as _np
    import concourse.bacc as _bacc
    from concourse import mybir as _mybir
    from concourse.bass_utils import run_bass_kernel_spmd as _run

    nc = _bacc.Bacc("TRN2", target_bir_lowering=False, num_devices=1)
    arrays, args = {}, []
    for name in _INS:
        a = _np.ascontiguousarray(inputs[name])
        arrays[f"in_{name}"] = a
        args.append(nc.dram_tensor(f"in_{name}", a.shape, _mybir.dt.from_np(a.dtype), kind="ExternalInput").ap())
    args.append(nc.dram_tensor("out_0", inputs["x"].shape, F32, kind="ExternalOutput").ap())
    gnn_ffn_mamba_kernel(nc, *args)
    r = _run(nc, [arrays], core_ids=[0])
    return r.results[0]["out_0"]
```

```python
from contextlib import ExitStack

import numpy as np

import concourse.bass as bass
from concourse import mybir

ALU = mybir.AluOpType
ACT = mybir.ActivationFunctionType
F32 = mybir.dt.float32
I32 = mybir.dt.int32
AX_X = mybir.AxisListType.X

P = 128
EPS = 1e-5
ALPHA = 0.2
NEG = 9.0e15
GELU_CUBE = 0.044715
GELU_SCALE = 0.7978845608028654

STEPS = {
    "tensor": [
        ("b_res", 1), ("b_bcast", 1), ("q_ffn2", 2), ("b_pturn", 1), ("q_scatter", 2), ("b_att", 1),
        ("m_xbc_a", 3), ("a_turn", 0), ("m_xbc_b", 3), ("m_da", 3), ("g_turn", 2), ("a_mlp1.0", 0),
        ("g_proj", 2), ("a_mlp1.1", 0), ("g_bcast", 2), ("m_cum_col", 3), ("a_fc.0", 0), ("a_fc.1", 0),
        ("a_bcast", 0), ("m_cb", 3), ("g_pturn", 2), ("q_route", 1), ("m_xrow", 3), ("g_att", 2),
        ("a_att.0", 0), ("a_att.1", 0), ("q_gather", 1), ("q_ffn1.0", 1), ("m_y.0", 3), ("m_y.1", 3),
        ("a_uturn", 0), ("q_ffn1.1", 1), ("m_yturn", 3), ("a_mlp2", 0), ("m_out", 3), ("m_turn", 2),
        ("b_proj", 0), ("m_z", 2),
    ],
    "scalar": [
        ("b_proj", 1), ("m_z", 3), ("m_dt_exp", 3), ("b_exp", 1), ("b_pturn", 1), ("b_att", 1), ("b_elu_b", 1),
        ("a_turn", 0), ("m_xbc_a", 3), ("m_xbc_b", 3), ("g_turn", 2), ("g_proj", 2), ("a_mlp1", 0),
        ("m_silu", 3), ("g_exp", 2), ("g_pturn", 2), ("a_factors", 0), ("q_route", 1), ("a_fcol", 0),
        ("m_xrow", 3), ("m_decay.0", 3), ("g_att", 2), ("a_att", 0), ("q_gather", 1), ("m_decay.1", 3),
        ("a_elu_b", 0), ("m_yturn", 3), ("q_gelu_a", 1), ("m_gated", 3), ("a_mlp2", 0), ("m_turn", 2),
        ("q_gelu_c", 1),
    ],
    "vector": [
        ("q_ffn2", 2), ("b_proj", 1), ("a_stats", 0), ("b_mask", 1), ("b_lrelu", 1), ("b_max", 1),
        ("q_scatter", 2), ("m_gate", 3), ("b_pturn", 1), ("q_x2", 2), ("g_stats", 2), ("a_norm", 0),
        ("b_elu_c", 1), ("g_norm", 2), ("b_x1", 1), ("m_scan", 3), ("q_stats", 1), ("m_conv_b.0", 3),
        ("g_proj", 2), ("m_conv_b.1", 3), ("g_mask", 2), ("m_conv_b.2", 3), ("g_lrelu", 2), ("q_norm", 1),
        ("a_fc", 0), ("m_cum_col", 3), ("g_max", 2), ("m_silu", 3), ("a_fcol", 0), ("q_route", 1),
        ("g_pturn", 2), ("a_maxima", 0), ("m_decay.0", 3), ("a_probs", 0), ("q_route_col", 1), ("m_cb", 3),
        ("q_rank", 1), ("a_att", 0), ("m_decay.1", 3), ("m_mix.0", 3), ("m_mix.1", 3), ("a_elu_c", 0),
        ("g_elu_b", 2), ("m_y.0", 3), ("m_y.1", 3), ("a_uturn", 0), ("g_x3", 2), ("m_stats", 2),
        ("q_gelu_a", 1), ("m_norm", 2), ("q_gelu_b", 1), ("m_out", 3),
    ],
    "gpsimd": [
        ("m_dt", 3), ("a_norm", 0), ("m_dt_log", 3), ("b_elu_a", 1), ("g_norm", 2), ("m_da", 3),
        ("m_conv_a", 3), ("q_norm", 1), ("q_turn", 1), ("m_xrow", 3), ("a_elu_a", 0), ("g_elu_a", 2),
        ("m_turn", 3), ("m_norm", 2), ("q_gelu_b", 1), ("m_rms", 3),
    ],
    "sync": [
        ("a_load", 0), ("m_spread", 3), ("a_residual", 0), ("m_store", 3),
    ],
}


def log1p_coefficients(degree):
    nodes = (1 + np.cos(np.pi * (np.arange(64) + 0.5) / 64)) / 18
    root = np.sqrt(nodes)
    return [float(c) for c in np.polynomial.polynomial.polyfit(nodes, np.arctanh(root) / root, degree)]


def gnn_ffn_mamba_kernel(nc, x, adj, mlp1_w, mlp1_b, mlp2_w, mlp2_b, W_fc, a_fc, W_hand, a_hand,
                         wr, br, w1, b1, w2, b2, gW, ga, W_in, conv_w, conv_b, dt_bias, A_log, D_skip,
                         norm_w, W_out, W_lin, b_lin, out):
    B, N, D = x.shape
    H = mlp1_w.shape[1]
    F = w1.shape[1]
    DI = W_out.shape[0]
    NH = D_skip.shape[0]
    HD = DI // NH
    DS = (conv_w.shape[0] - DI) // 2
    TAPS = conv_w.shape[1]
    U = N // P
    KD = D // P
    KH = H // P
    KF = F // P
    KI = DI // P
    KX = KI + 1
    TOPK = max(1, int(0.5 * N)) - 1
    PAD = TAPS - 1
    XBC = DI + 2 * DS
    Z0, DT0, Z1, X0 = 0, D, D + NH, DI + NH
    assert U == 2 and KD == 2 and KH == 4 and KI == 4 and 2 * DS == P and TOPK < P and TAPS == 4
    LOG = log1p_coefficients(4)

    with ExitStack() as ctx:
        def sb(name, shape, dt=F32):
            return ctx.enter_context(nc.sbuf_tensor(name, shape, dt))

        def bank(name):
            return ctx.enter_context(nc.psum_tensor(name, [P, 512], F32))

        def sem(name):
            return ctx.enter_context(nc.semaphore(name))

        w_mlp1 = sb("w_mlp1", [P, KD, H])
        c_mlp1 = sb("c_mlp1", [P, KH])
        w_fc = sb("w_fc", [P, KH, H // D, D + 2])
        w_mlp2 = sb("w_mlp2", [P, KH, D])
        c_mlp2 = sb("c_mlp2", [P, KD])
        w_hand = sb("w_hand", [P, KD, D + 2])
        w_gat = sb("w_gat", [P, KD, D + 2])
        w_route = sb("w_route", [P, D])
        c_route = sb("c_route", [P, 1])
        w_up = sb("w_up", [P, KD, F])
        c_up = sb("c_up", [P, KF])
        w_down = sb("w_down", [P, KF, D])
        c_down = sb("c_down", [P, D])
        w_in = sb("w_in", [P, KD, W_in.shape[1]])
        w_conv = sb("w_conv", [P, KX, TAPS])
        c_conv = sb("c_conv", [P, KX])
        c_dt = sb("c_dt", [P, U, NH])
        a_row = sb("a_row", [P, U, NH])
        d_row = sb("d_row", [P, NH])
        n_col = sb("n_col", [P, KI])
        w_comb = sb("w_comb", [P, KI, D])
        c_lin = sb("c_lin", [P, D])
        ident = sb("ident", [P, P])
        ones = sb("ones", [P, N])
        causal = sb("causal", [P, N + P])
        earlier = sb("earlier", [P, U, N])
        slot_i = sb("slot_i", [P, P], I32)
        slot = sb("slot", [P, P])
        power = sb("power", [P, U])
        epsilon = sb("epsilon", [P, U])
        gate_cols = sb("gate_cols", [P, 32])
        hold_cols = sb("hold_cols", [P, 4])
        inverse = sb("inverse", [P, U * NH])
        twos = sb("twos", [P, U * NH])
        log_c = sb("log_c", [P, len(LOG), U * NH])
        mask0 = sb("mask0", [P, U, N])
        mask1 = sb("mask1", [P, U, N])

        x_in = sb("x_in", [P, U, D])
        x0 = sb("x0", [P, U, D])
        x1 = sb("x1", [P, U, D])
        x2 = sb("x2", [P, U, D])
        x3 = sb("x3", [P, U, D])
        bn = {k: sb(f"bn_{k}", [P, U, 6]) for k in "aqgm"}
        mv = {k: sb(f"mv_{k}", [P, U, 2]) for k in "aqgm"}
        var = {k: sb(f"var_{k}", [P, U]) for k in "aqgm"}
        rstd = {k: sb(f"rstd_{k}", [P, U]) for k in "aqgm"}
        xn = {k: sb(f"xn_{k}", [P, U, D]) for k in "aqgm"}
        xT = {k: sb(f"xT_{k}", [P, KD, N]) for k in "agm"}

        o1T = sb("o1T", [P, KH, N])
        h1 = sb("h1", [P, U, H // D, D + 2])
        f1 = sb("f1", [P, U, 2])
        top = sb("top", [P, 1])
        arg = sb("arg", [P, N])
        fac = sb("fac", [P, 2, N])
        args = fac
        gcol = sb("gcol", [P, U])
        bcol = sb("bcol", [P, U])
        dcol = sb("dcol", [P, U])
        low = sb("low", [P, U, N])
        p1 = low
        r1 = sb("r1", [P, U])
        e1 = sb("e1", [P, U, H])
        e1m = e1x = e1
        u1 = sb("u1", [P, U, H])
        z1T = e1[:, :, :].rearrange("p u (h n) -> p (u h) n", n=N)
        o2T = sb("o2T", [P, KD, N])

        hp = {k: sb(f"hp_{k}", [P, U, D]) for k in "bg"}
        fc = {k: sb(f"fc_{k}", [P, U, 2]) for k in "bg"}
        sc = {k: sb(f"sc_{k}", [P, U, N]) for k in "bg"}
        nmax = {k: sb(f"nmax_{k}", [P, U]) for k in "bg"}
        lr = pr = sc
        rs = {k: sb(f"rs_{k}", [P, U]) for k in "bg"}
        rr = {k: sb(f"rr_{k}", [P, U]) for k in "bg"}
        pT = {k: sb(f"pT_{k}", [P, U, N]) for k in "bg"}
        ea = {k: sb(f"ea_{k}", [P, U, D]) for k in "bg"}
        eb = ea
        ec = ea["b"]
        ue = {k: sb(f"ue_{k}", [P, U, D]) for k in "bg"}
        v1 = ue["b"]

        wrow = sb("wrow", [P, N])
        wsum = sb("wsum", [P, U])
        wcol = sb("wcol", [P, U])
        junk = sb("junk", [P, N])
        above = sb("above", [P, U])
        ties = sb("ties", [P, U])
        rank = sb("rank", [P, U])
        pick = sb("pick", [P, U, P])
        pickT = sb("pickT", [P, N])
        selT = sb("selT", [P, KD, P])
        ga_ = sb("ga_", [P, KF, P])
        gsq = sb("gsq", [P, KF, P])
        gpl = gq = gt = gl = gsq
        yff = sb("yff", [P, D])
        xs = sb("xs", [P, U, D])

        xbc = sb("xbc", [P, KX, PAD + N])
        acc = sb("acc", [P, KX, N])
        th = sb("th", [P, KX, N])
        xc = acc
        bT = sb("bT", [DS, N])
        cT = sb("cT", [DS, N])
        dt_raw = sb("dt_raw", [P, U * NH])
        dt_a = sb("dt_a", [P, U * NH])
        dt_e = sb("dt_e", [P, U * NH])
        dt_p = sb("dt_p", [P, U * NH])
        dt_w = [sb(f"dt_w{i}", [P, U * NH]) for i in range(14)]
        dt = sb("dt", [P, U, NH])
        dt8 = sb("dt8", [P, U, NH])
        dA = sb("dA", [P, U, NH])
        cumT = sb("cumT", [P, N])
        cumcol = sb("cumcol", [P, U, NH])
        cumB = sb("cumB", [P, NH, N])
        dec0 = sb("dec0", [P, NH, N])
        dec1 = sb("dec1", [P, NH, P])
        cb = sb("cb", [P, N + P])
        tz = sb("tz", [P, U, DI])
        gz = yg = tz
        xdt = sb("xdt", [P, U, DI])
        xr = sb("xr", [P, U, DI])
        ysq = th[:, 0:KI, :].rearrange("p (u h) n -> p u (h n)", u=U)
        ss = sb("ss", [P, U])
        ms = sb("ms", [P, U])
        rms = sb("rms", [P, U])
        ygT = xdt[:, :, :].rearrange("p u (h n) -> p (u h) n", n=N)
        x3b = sb("x3b", [P, U, D])
        x4 = x3b
        cum_dram = nc.dram_tensor("cum_dram", [NH, N], F32, kind="Internal").ap()

        A0, A1, A2 = bank("A0"), bank("A1"), bank("A2")
        Q0, Q1 = bank("Q0"), bank("Q1")
        M0, M1, M2 = bank("M0"), bank("M1"), bank("M2")

        def two(b):
            return b[:, :].rearrange("p (u n) -> p u n", u=2)

        def rows1(half, u, extra=0):
            return (A0, A1)[u][:, 0:D + extra] if half == 0 else A2[:, u * D:(u + 1) * D]

        NAMES = """a_stats a_rstd a_xn a_xT_ps a_xT  q_stats q_rstd q_xn
            g_stats g_rstd g_xn g_xT_ps g_xT  m_stats m_rstd m_xn m_xT_ps m_xT
            o1_ps o1_ready h1_ps h1_a h1_b f1_ready fb_ps top_ready gcol_ready
            arg_ready args_ready fac_ready bd_ready low_ready p1_ready y1_ps r1_ready e1_ready e1m_ready
            e1x_ready u1_ready u1T_ps z1_ready o2_ps o2_ready x1_ready
            b_h_ps b_hp b_fc b_fb_ps b_sc b_lr b_nmax b_pr b_pT_ps b_pT b_rr b_y_ps b_ea b_eb b_ec b_ue
            res_ps v1_ready
            g_h_ps g_hp g_fc g_fb_ps g_sc g_lr g_nmax g_pr g_pT_ps g_pT g_rr g_y_ps g_ea g_eb g_ue
            wsum_ready w_ps wrow_ready wcol_ready counts_ready rank_ready pick_ready sel_ps sel_ready
            up_ps ga_ready gsq_ready gpl_ready gq_ready gt_ready gl_ready yff_ps yff_ready sc_ps xs_ready
            x2_ready x3_ready
            xbc_ps xbc_ready acc_ready conv th_ready xc_ready
            dt_copied dt_a_ready dt_abs dt_e_ready dt_chain dt_ready dA_ps cumT_ready cumc_ps cumcol_ready
            cb_ps cb_ready z_ps tz_ready gz_ready xr_ps xr_ready xdt_ready dx_ready decarg_ready dec_ready mix_ready
            y_ps ysum yg_ready ss_ready da_ready rms_ready yT_ps yT_ready out_ps x3b_ready x4_ready"""
        S = {name: sem(name) for name in NAMES.split()}
        x_loaded = sem("x_loaded")
        x0_loaded = sem("x0_loaded")
        cum_stored = sem("cum_stored")
        cum_spread = sem("cum_spread")
        out_stored = sem("out_stored")
        consts = sem("consts")

        setup_sem = [sem(f"setup{i}") for i in range(5)]
        DV, PL, PEs, AC, LD = setup_sem
        adj_i = xbc[:, 0:2, 0:N]
        adj_f = th[:, 0:2, :]
        a_fc_b = e1
        a_hand_b = u1
        a_gat_b = yg
        w_out_s = dec0[:, 0:KI, 0:D]
        w_outT = dec0[:, KI:KI + KD + 2, 0:D]
        w_lin_s = ygT[:, 0:KD, 0:D]
        a_log_s = dt_a[:, 0:NH]

        with nc.Block() as setup:
            loads = []

            def col(v, k):
                return v.rearrange("(k p) -> p k", p=P)

            def row(v):
                return v.rearrange("(a n) -> a n", a=1).partition_broadcast(P).rearrange("q a n -> q (a n)")

            loads.append((adj_i.bitcast(I32), adj.rearrange("(u p) n -> p u n", p=P)))
            loads.append((w_mlp1[:], mlp1_w.rearrange("(k p) n -> p k n", p=P)))
            for half in range(H // D):
                loads.append((w_fc[:, :, half, 0:D],
                              W_fc[:, half * D:(half + 1) * D].rearrange("(k p) n -> p k n", p=P)))
            loads.append((w_mlp2[:], mlp2_w.rearrange("(k p) n -> p k n", p=P)))
            loads.append((w_hand[:, :, 0:D], W_hand.rearrange("(k p) n -> p k n", p=P)))
            loads.append((w_gat[:, :, 0:D], gW.rearrange("(k p) n -> p k n", p=P)))
            loads.append((w_up[:], w1.rearrange("(k p) n -> p k n", p=P)))
            loads.append((w_down[:], w2.rearrange("(k p) n -> p k n", p=P)))
            for at, start, width in ((Z0, 0, D), (DT0, DI + XBC, NH), (Z1, D, DI - D), (X0, DI, XBC)):
                loads.append((w_in[:, :, at:at + width],
                              W_in[:, start:start + width].rearrange("(k p) n -> p k n", p=P)))
            loads.append((w_out_s, W_out.rearrange("(k p) n -> p k n", p=P)))
            loads.append((w_lin_s, W_lin.rearrange("(k p) n -> p k n", p=P)))
            loads.append((w_conv[:], conv_w.rearrange("(k p) t -> p k t", p=P)))
            loads.append((a_fc_b[:], a_fc.rearrange("(s n) o -> (n o) s", s=1).rearrange("n s -> s n")
                          .partition_broadcast(P).rearrange("q s (h n) -> q (s h) n", h=2)))
            loads.append((a_hand_b[:, 0, :], a_hand.rearrange("n o -> o n").partition_broadcast(P)
                          .rearrange("q o n -> q (o n)")))
            loads.append((a_gat_b[:, 0, :], ga.rearrange("n o -> o n").partition_broadcast(P)
                          .rearrange("q o n -> q (o n)")))
            loads.append((w_route[:], row(wr.rearrange("n o -> (n o)"))))
            loads.append((c_mlp1[:], col(mlp1_b, KH)))
            loads.append((c_mlp2[:], col(mlp2_b, KD)))
            loads.append((c_up[:], col(b1, KF)))
            loads.append((c_conv[:], col(conv_b, KX)))
            loads.append((n_col[:], col(norm_w, KI)))
            loads.append((c_route[:], row(br)))
            loads.append((c_down[:], row(b2)))
            loads.append((c_lin[:], row(b_lin)))
            for u in range(U):
                loads.append((c_dt[:, u, :], row(dt_bias)))
            loads.append((a_log_s, row(A_log)))
            loads.append((d_row[:], row(D_skip)))

            @setup.sync
            def _(sp):
                with nc.allow_non_contiguous_dma("parameters, once"):
                    for dst, src in loads:
                        sp.dma_start(dst, src).then_inc(LD, 16)

            @setup.gpsimd
            def _(pool):
                nc.gpsimd.memset(ident[:], 0.0)
                nc.gpsimd.memset(ones[:], 1.0)
                nc.gpsimd.memset(causal[:], 1.0)
                nc.gpsimd.memset(earlier[:], 1.0)
                nc.gpsimd.memset(power[:], -0.5)
                nc.gpsimd.memset(epsilon[:], EPS)
                nc.gpsimd.memset(inverse[:], -1.0)
                nc.gpsimd.memset(twos[:], 2.0)
                for i, c in enumerate(LOG):
                    nc.gpsimd.memset(log_c[:, i, :], 2.0 * c)
                nc.gpsimd.memset(cumT[:], 0.0)
                nc.gpsimd.iota(slot_i[:], pattern=[[1, P]], base=0, channel_multiplier=0).then_inc(PL, 1)
                pool.wait_ge(PL, 1)
                nc.gpsimd.affine_select(out=ident[:], in_=ident[:], compare_op=ALU.not_equal, fill=1.0, base=0,
                                        pattern=[[-1, P]], channel_multiplier=1)
                nc.gpsimd.affine_select(out=causal[:, 0:N], in_=causal[:, 0:N], compare_op=ALU.is_ge, fill=0.0,
                                        base=0, pattern=[[1, N]], channel_multiplier=-1)
                nc.gpsimd.affine_select(out=causal[:, N:], in_=causal[:, N:], compare_op=ALU.is_ge, fill=0.0,
                                        base=0, pattern=[[1, P]], channel_multiplier=-1)
                nc.gpsimd.affine_select(out=earlier[:], in_=earlier[:], compare_op=ALU.is_gt, fill=0.0, base=0,
                                        pattern=[[P, U], [-1, N]], channel_multiplier=1)
                nc.gpsimd.tensor_copy(slot[:], slot_i[:]).then_inc(PL, 1)
                pool.wait_ge(PL, 2)
                nc.gpsimd.memset(slot[:, TOPK:], -1.0).then_inc(PL, 1)

            @setup.vector
            def _(v):
                n = [0]

                def done(ins):
                    n[0] += 1
                    ins.then_inc(DV, 1)

                def settle():
                    v.wait_ge(DV, n[0])

                v.wait_ge(LD, 16 * len(loads))
                v.wait_ge(PL, 3)
                done(nc.vector.tensor_scalar(adj_f, adj_i.bitcast(I32), 0, None, ALU.is_gt))
                settle()
                done(nc.vector.tensor_scalar(mask0[:], adj_f, -1.0, NEG, ALU.add, ALU.mult))
                settle()
                done(nc.vector.tensor_reduce(rs["g"][:], adj_f, AX_X, ALU.add))
                settle()
                done(nc.vector.reciprocal(rr["g"][:], rs["g"][:]))
                settle()
                done(nc.vector.tensor_scalar(nmax["g"][:], rr["g"][:], 0.0, None, ALU.mult))
                settle()
                for u in range(U):
                    done(nc.vector.tensor_scalar(mask1[:, u, :], mask0[:, u, :], nmax["g"][:, u:u + 1], None, ALU.add))
                def attend(weights, column, a_half, spare):
                    done(nc.vector.scalar_tensor_tensor(out=spare, in0=weights, scalar=1.0, in1=a_half, op0=ALU.mult,
                                                        op1=ALU.mult, accum_out=column))
                    settle()

                for half in range(2):
                    for t in range(KH):
                        attend(w_fc[:, t, :, 0:D], w_fc[:, t, 0, D + half:D + half + 1],
                               a_fc_b[:, half, :].rearrange("p (a n) -> p a n", n=D), p1[:])
                    for w, a_b in ((w_hand, a_hand_b), (w_gat, a_gat_b)):
                        for t in range(KD):
                            attend(w[:, t, 0:D], w[:, t, D + half:D + half + 1],
                                   a_b[:, 0, half * D:(half + 1) * D], p1[:, 0, :])
                done(nc.vector.tensor_scalar(d_row[:], d_row[:], 0.5, None, ALU.mult))
                done(nc.vector.memset(h1[:, :, 0, D:D + 1], 1.0))
                done(nc.vector.tensor_scalar(w_down[:], w_down[:], 0.5, None, ALU.mult))
                v.wait_ge(AC, 1)
                for u in range(U):
                    done(nc.vector.tensor_scalar(a_row[:, u, :], dt_e[:, 0:NH], -1.0, None, ALU.mult))
                for m in range(KD):
                    v.wait_ge(PEs, m + 1)
                    done(nc.vector.tensor_copy(w_outT[:, 2 * m:2 * m + 2, :].rearrange("p a n -> p (a n)"),
                                               (A0, A1)[m][:, :]))
                v.wait_ge(PEs, KD + 1)
                for t in range(KI):
                    done(nc.vector.tensor_scalar(w_comb[:, t, :], (M0, M1)[t // 2][:, (t % 2) * D:(t % 2 + 1) * D],
                                                 n_col[:, t:t + 1], None, ALU.mult))
                settle()
                nc.vector.memset(xbc[:, :, 0:PAD], 0.0).then_inc(consts, 1)

            DV_TURNED = 2 + 3 + U + 2 * (KH + KD + KD) + 2 + 1 + U + KD

            @setup.scalar
            def _(act):
                act.wait_ge(LD, 16 * len(loads))
                nc.scalar.activation(dt_e[:, 0:NH], a_log_s, ACT.Exp).then_inc(AC, 1)

            @setup.tensor
            def _(pe):
                pe.wait_ge(LD, 16 * len(loads))
                pe.wait_ge(PL, 3)
                for m in range(KD):
                    for t in range(KI):
                        last = nc.tensor.transpose((A0, A1)[m][:, t * P:(t + 1) * P],
                                                   w_out_s[:, t, m * P:(m + 1) * P], ident[:])
                    last.then_inc(PEs, 1)
                pe.wait_ge(DV, DV_TURNED)
                wT = w_outT.rearrange("p (m a) n -> p m (a n)", m=KD)
                for t in range(KI):
                    for m in range(KD):
                        last = nc.tensor.matmul((M0, M1)[t // 2][:, (t % 2) * D:(t % 2 + 1) * D],
                                                wT[:, m, t * P:(t + 1) * P], w_lin_s[:, m, :],
                                                start=(m == 0), stop=(m == KD - 1))
                last.then_inc(PEs, 1)

        def turns(eng, name, steps):
            order = STEPS[name]
            assert sorted(step for step, _ in order) == sorted(steps)
            last = max(lag for _, lag in order)

            def turn(t):
                for step, lag in order:
                    b = t - lag
                    if not (isinstance(b, int) and not 1 <= b <= B):
                        steps[step](b)

            for t in range(1, last + 2):
                turn(t)
            with eng.Fori(last + 2, B + 1) as t:
                turn(t)
            for t in range(B + 1, B + last + 1):
                turn(t)

        def parts(name, step, count):
            return {f"{name}.{i}": lambda b, i=i: step(b, i) for i in range(count)}

        def nth(b, per, i):
            return b * per - (per - i)

        def before(eng, semaphore, b):
            if not (isinstance(b, int) and b < 2):
                eng.wait_ge(semaphore, b - 1)

        block = ctx.enter_context(nc.Block())

        @block.sync
        def _(sp):
            def a_load(b):
                before(sp, S["a_xn"], b)
                sp.dma_start(x_in[:], x[b - 1].rearrange("(u p) d -> p u d", p=P)).then_inc(x_loaded, 16)

            def a_residual(b):
                before(sp, S["x1_ready"], b)
                sp.dma_start(x0[:], x[b - 1].rearrange("(u p) d -> p u d", p=P)).then_inc(x0_loaded, 16)

            def m_spread(b):
                sp.wait_ge(S["cumT_ready"], b)
                sp.dma_start(cum_dram, cumT[0:NH, :]).then_inc(cum_stored, 16)
                sp.wait_ge(cum_stored, 16 * b)
                sp.dma_start(cumB[:], cum_dram.partition_broadcast(P)).then_inc(cum_spread, 16)

            def m_store(b):
                sp.wait_ge(S["x4_ready"], b)
                sp.dma_start(out[b - 1].rearrange("(u p) d -> p u d", p=P), x4[:]).then_inc(out_stored, 16)

            turns(sp, "sync", dict(a_load=a_load, a_residual=a_residual, m_spread=m_spread, m_store=m_store))
            sp.wait_ge(cum_stored, 16 * B)
            sp.wait_ge(out_stored, 16 * B)

        @block.gpsimd
        def _(pool):
            GATES = {}

            def after(semaphore, b):
                pool.wait_ge(semaphore, b)

            def gate(semaphore, b, part=0):
                after(semaphore, b)
                c = GATES.setdefault((semaphore.name, part), len(GATES))
                nc.gpsimd.tensor_tensor(gate_cols[:, c:c + 1], ones[:, 0:1], ones[:, 0:1], ALU.add)

            def rstd_of(k):
                def step(b):
                    after(S[f"{k}_stats"], nth(b, 2, 2))
                    nc.gpsimd.tensor_tensor(var[k][:], mv[k][:, :, 1], epsilon[:], ALU.add).then_inc(S[f"{k}_rstd"], 1)
                    after(S[f"{k}_rstd"], nth(b, 2, 1))
                    nc.gpsimd.tensor_tensor(rstd[k][:], var[k][:], power[:], ALU.pow).then_inc(S[f"{k}_rstd"], 1)
                return step

            def a_elu_a(b):
                gate(S["e1_ready"], b)
                nc.gpsimd.tensor_scalar(e1m[:], e1[:], 1.0, None, ALU.min).then_inc(S["e1m_ready"], 1)

            def clip(k):
                def step(b):
                    gate(S[f"{k}_ea"], b)
                    nc.gpsimd.tensor_scalar(eb[k][:], ea[k][:], 1.0, None, ALU.min).then_inc(S[f"{k}_eb"], 1)
                return step

            def q_turn(b):
                if not (isinstance(b, int) and b < 2):
                    gate(S["x2_ready"], b - 1)
                after(S["q_xn"], b)
                nc.gpsimd.tensor_tensor(xs[:], x1[:], xn["q"][:], ALU.add).then_inc(S["xs_ready"], 1)

            def q_gelu_b(b):
                gate(S["gsq_ready"], b)
                nc.gpsimd.tensor_scalar(gpl[:], gsq[:], GELU_CUBE, 1.0, ALU.mult, ALU.add).then_inc(S["gpl_ready"], 1)

            def m_turn(b):
                if not (isinstance(b, int) and b < 2):
                    gate(out_stored, 16 * (b - 1))
                after(S["m_xn"], b)
                nc.gpsimd.tensor_tensor(x3b[:], x3[:], c_lin[:, None, :].to_broadcast([P, U, D]),
                                        ALU.add).then_inc(S["x3b_ready"], 1)

            def m_dt(b):
                after(S["dt_copied"], b)
                nc.gpsimd.tensor_tensor(dt_a[:], dt_raw[:], c_dt[:, :, :].rearrange("p u h -> p (u h)"),
                                        ALU.add).then_inc(S["dt_a_ready"], 1)

            CHAIN = 13

            def m_dt_log(b):
                gate(S["dt_e_ready"], b)
                w = dt_w
                links = [
                    lambda: nc.gpsimd.tensor_tensor(w[0][:], dt_e[:], twos[:], ALU.add),
                    lambda: nc.gpsimd.tensor_tensor(w[1][:], w[0][:], inverse[:], ALU.pow),
                    lambda: nc.gpsimd.tensor_tensor(w[2][:], dt_e[:], w[1][:], ALU.mult),
                    lambda: nc.gpsimd.tensor_tensor(w[3][:], w[2][:], w[2][:], ALU.mult),
                    lambda: nc.gpsimd.tensor_tensor(w[4][:], log_c[:, 4, :], w[3][:], ALU.mult),
                    lambda: nc.gpsimd.tensor_tensor(w[5][:], w[4][:], log_c[:, 3, :], ALU.add),
                    lambda: nc.gpsimd.tensor_tensor(w[6][:], w[5][:], w[3][:], ALU.mult),
                    lambda: nc.gpsimd.tensor_tensor(w[7][:], w[6][:], log_c[:, 2, :], ALU.add),
                    lambda: nc.gpsimd.tensor_tensor(w[8][:], w[7][:], w[3][:], ALU.mult),
                    lambda: nc.gpsimd.tensor_tensor(w[9][:], w[8][:], log_c[:, 1, :], ALU.add),
                    lambda: nc.gpsimd.tensor_tensor(w[10][:], w[9][:], w[3][:], ALU.mult),
                    lambda: nc.gpsimd.tensor_tensor(w[11][:], w[10][:], log_c[:, 0, :], ALU.add),
                    lambda: nc.gpsimd.tensor_tensor(w[12][:], w[11][:], w[2][:], ALU.mult),
                ]
                assert len(links) == CHAIN
                for i, link in enumerate(links):
                    if i:
                        pool.wait_ge(S["dt_chain"], nth(b, CHAIN, i))
                    link().then_inc(S["dt_chain"], 1)
                after(S["dt_chain"], b * CHAIN)
                nc.gpsimd.tensor_tensor(dt[:, :, :].rearrange("p u h -> p (u h)"), w[12][:], dt_p[:],
                                        ALU.add).then_inc(S["dt_ready"], 1)

            def m_da(b):
                after(S["dt_ready"], b)
                nc.gpsimd.tensor_tensor(dA[:], dt[:], a_row[:], ALU.mult)
                nc.gpsimd.tensor_scalar(dt8[:], dt[:], 0.125, None, ALU.mult).then_inc(S["da_ready"], 1)

            def m_conv_a(b):
                for c, i in ((4, 1), (0, 2), (2, 3)):
                    gate(S["xbc_ready"], nth(b, 3, i), i)
                    for k in range(c, min(c + 2, KX)):
                        last = nc.gpsimd.tensor_scalar(acc[:, k, :], xbc[:, k, PAD:PAD + N],
                                                       w_conv[:, k, PAD:PAD + 1], c_conv[:, k:k + 1],
                                                       ALU.mult, ALU.add)
                last.then_inc(S["acc_ready"], 1)

            def m_xrow(b):
                after(S["xr_ready"], b)
                heads = xr[:, :, :].rearrange("p u (h d) -> p (u h) d", h=NH)
                nc.gpsimd.tensor_tensor(xdt[:, :, :].rearrange("p u (h d) -> p (u h) d", h=NH), heads,
                                        dt8[:, :, :].rearrange("p u h -> p (u h)")[:, :, None]
                                        .to_broadcast([P, U * NH, HD]), ALU.mult).then_inc(S["xdt_ready"], 1)
                after(S["xdt_ready"], b)
                for u in range(U):
                    last = nc.gpsimd.tensor_tensor(xr[:, u, :].rearrange("p (h d) -> p h d", h=NH),
                                                   xr[:, u, :].rearrange("p (h d) -> p h d", h=NH),
                                                   d_row[:, :, None].to_broadcast([P, NH, HD]), ALU.mult)
                last.then_inc(S["dx_ready"], 1)

            def m_rms(b):
                gate(S["ss_ready"], b)
                nc.gpsimd.tensor_scalar(ms[:], ss[:], 1.0 / DI, 4.0 * EPS, ALU.mult, ALU.add)\
                    .then_inc(S["rms_ready"], 1)
                after(S["rms_ready"], nth(b, 2, 1))
                nc.gpsimd.tensor_tensor(rms[:], ms[:], power[:], ALU.pow).then_inc(S["rms_ready"], 1)

            turns(nc.gpsimd, "gpsimd", dict(
                a_norm=rstd_of("a"), q_norm=rstd_of("q"), g_norm=rstd_of("g"), m_norm=rstd_of("m"),
                a_elu_a=a_elu_a, b_elu_a=clip("b"), g_elu_a=clip("g"), q_turn=q_turn, q_gelu_b=q_gelu_b,
                m_turn=m_turn, m_dt=m_dt, m_dt_log=m_dt_log, m_da=m_da, m_conv_a=m_conv_a, m_xrow=m_xrow,
                m_rms=m_rms))

        @block.scalar
        def _(act):
            def evac_T(k, src):
                def step(b):
                    act.wait_ge(S[f"{k}_xT_ps"], b)
                    nc.scalar.copy(xT[k][:], two(src)).then_inc(S[f"{k}_xT"], 1)
                return step

            def a_mlp1(b):
                for ps, i, m0 in ((A1, 1, 0), (A2, 2, 2)):
                    act.wait_ge(S["o1_ps"], nth(b, 2, i))
                    for m in (m0, m0 + 1):
                        last = nc.scalar.activation(o1T[:, m, :], ps[:, (m - m0) * N:(m - m0 + 1) * N], ACT.Relu,
                                                    bias=c_mlp1[:, m:m + 1])
                last.then_inc(S["o1_ready"], 1)

            def a_fcol(b):
                act.wait_ge(S["f1_ready"], b)
                for u in range(U):
                    last = nc.scalar.activation(h1[:, u, 0, 0:D], (A0, A1)[u][:, 0:D], ACT.Identity, bias=1.0)
                last.then_inc(S["h1_a"], 1)

            def a_factors(b):
                act.wait_ge(S["gcol_ready"], b)
                nc.scalar.activation(bcol[:], gcol[:], ACT.Exp)
                nc.scalar.activation(dcol[:], gcol[:], ACT.Exp, scale=ALPHA).then_inc(S["bd_ready"], 1)
                act.wait_ge(S["args_ready"], b)
                nc.scalar.activation(fac[:], args[:], ACT.Exp).then_inc(S["fac_ready"], 1)
                act.wait_ge(S["fac_ready"], b)
                act.wait_ge(S["bd_ready"], b)
                for u in range(U):
                    last = nc.scalar.activation(low[:, u, :], fac[:, 1, :], ACT.Copy, scale=dcol[:, u:u + 1])
                last.then_inc(S["low_ready"], 1)

            def a_att(b):
                act.wait_ge(S["r1_ready"], b)
                for half in range(H // D):
                    act.wait_ge(S["y1_ps"], nth(b, 2, half + 1))
                    for u in range(U):
                        last = nc.scalar.activation(e1[:, u, half * D:(half + 1) * D], rows1(half, u), ACT.Exp,
                                                    bias=-1.0, scale=r1[:, u:u + 1])
                last.then_inc(S["e1_ready"], 1)

            def a_elu_b(b):
                act.wait_ge(S["e1m_ready"], b)
                nc.scalar.activation(e1x[:], e1m[:], ACT.Exp, bias=-1.0).then_inc(S["e1x_ready"], 1)

            def a_mlp2(b):
                act.wait_ge(S["o2_ps"], b)
                for m in range(KD):
                    last = nc.scalar.activation(o2T[:, m, :], A1[:, m * N:(m + 1) * N], ACT.Relu,
                                                bias=c_mlp2[:, m:m + 1])
                last.then_inc(S["o2_ready"], 1)

            def proj(k, banks):
                def step(b):
                    act.wait_ge(S[f"{k}_fc"], b)
                    for u in range(U):
                        last = nc.scalar.activation(hp[k][:, u, :], banks[u][:, 0:D], ACT.Identity, bias=1.0)
                    last.then_inc(S[f"{k}_hp"], 1)
                return step

            def softmax(k):
                def step(b):
                    act.wait_ge(S[f"{k}_nmax"], b)
                    for u in range(U):
                        last = nc.scalar.activation(pr[k][:, u, :], lr[k][:, u, :], ACT.Exp,
                                                    bias=nmax[k][:, u:u + 1], accum_out=rs[k][:, u:u + 1])
                    last.then_inc(S[f"{k}_pr"], 1)
                return step

            def pturn(k, ps):
                def step(b):
                    act.wait_ge(S[f"{k}_pT_ps"], b)
                    nc.scalar.copy(pT[k][:], two(ps)).then_inc(S[f"{k}_pT"], 1)
                return step

            def elu_exp(k, ps):
                def step(b):
                    act.wait_ge(S[f"{k}_y_ps"], b)
                    act.wait_ge(S[f"{k}_rr"], b)
                    for u in range(U):
                        last = nc.scalar.activation(ea[k][:, u, :], two(ps)[:, u, :], ACT.Exp, bias=-1.0,
                                                    scale=rr[k][:, u:u + 1])
                    last.then_inc(S[f"{k}_ea"], 1)
                return step

            def b_elu_b(b):
                act.wait_ge(S["b_eb"], b)
                nc.scalar.activation(ec[:], eb["b"][:], ACT.Exp, bias=-1.0).then_inc(S["b_ec"], 1)

            def q_route(b):
                act.wait_ge(S["w_ps"], b)
                nc.scalar.activation(wrow[:], Q0[:, 0:N], ACT.Identity, bias=c_route[:, 0:1])\
                    .then_inc(S["wrow_ready"], 1)

            def q_gather(b):
                act.wait_ge(S["sel_ps"], b)
                nc.scalar.copy(pickT[:], Q0[:, 0:N])
                nc.scalar.copy(selT[:], Q0[:, N:].rearrange("p (k r) -> p k r", k=KD)).then_inc(S["sel_ready"], 1)

            def q_gelu_a(b):
                act.wait_ge(S["ga_ready"], b)
                nc.scalar.activation(gsq[:], ga_[:], ACT.Square).then_inc(S["gsq_ready"], 1)

            def q_gelu_c(b):
                act.wait_ge(S["gq_ready"], b)
                nc.scalar.activation(gt[:], gq[:], ACT.Tanh, scale=GELU_SCALE).then_inc(S["gt_ready"], 1)

            def m_xbc_a(b):
                act.wait_ge(S["xbc_ps"], nth(b, 3, 1))
                nc.scalar.copy(xbc[:, 4, PAD:], M1[:, N:2 * N]).then_inc(S["xbc_ready"], 1)
                act.wait_ge(S["xbc_ps"], nth(b, 3, 2))
                nc.scalar.copy(xbc[:, 0:2, PAD:], two(M2)).then_inc(S["xbc_ready"], 1)

            def m_xbc_b(b):
                act.wait_ge(S["xbc_ps"], nth(b, 3, 3))
                nc.scalar.copy(xbc[:, 2:4, PAD:], two(M0)).then_inc(S["xbc_ready"], 1)

            def m_dt_exp(b):
                act.wait_ge(S["dt_a_ready"], b)
                nc.scalar.activation(dt_w[13][:], dt_a[:], ACT.Abs).then_inc(S["dt_abs"], 1)
                act.wait_ge(S["dt_abs"], b)
                nc.scalar.activation(dt_p[:], dt_a[:], ACT.Relu)
                nc.scalar.activation(dt_e[:], dt_w[13][:], ACT.Exp, scale=-1.0).then_inc(S["dt_e_ready"], 1)

            def m_silu(b):
                act.wait_ge(S["conv"], nth(b, 3, 3))
                before(act, S["ss_ready"], b)
                nc.scalar.activation(th[:], acc[:], ACT.Tanh, scale=0.5).then_inc(S["th_ready"], 1)

            def m_z(b):
                for u in range(U):
                    act.wait_ge(S["z_ps"], nth(b, 3, u + 1))
                    last = nc.scalar.copy(dt_raw[:, u * NH:(u + 1) * NH], (M1, M0)[u][:, D:D + NH])
                    if u == U - 1:
                        last.then_inc(S["dt_copied"], 1)
                    nc.scalar.activation(tz[:, u, 0:D], (M1, M0)[u][:, 0:D], ACT.Tanh, scale=0.5)\
                        .then_inc(S["tz_ready"], 1)
                act.wait_ge(S["z_ps"], nth(b, 3, 3))
                nc.scalar.activation(tz[:, :, D:], two(M2), ACT.Tanh, scale=0.5).then_inc(S["tz_ready"], 1)

            def m_xrow(b):
                for u in range(U):
                    act.wait_ge(S["xr_ps"], nth(b, 2, u + 1))
                    last = nc.scalar.copy(xr[:, u, :], (M2, M0)[u][:, :])
                last.then_inc(S["xr_ready"], 1)

            def m_decay(b, i):
                act.wait_ge(S["decarg_ready"], nth(b, 2, i + 1))
                dec = (dec0, dec1)[i]
                nc.scalar.activation(dec[:], dec[:], ACT.Exp).then_inc(S["dec_ready"], 1)

            def m_gated(b):
                for u in range(U):
                    act.wait_ge(S["yg_ready"], nth(b, 2, u + 1))
                    last = nc.scalar.activation(ysq[:, u, :], yg[:, u, :], ACT.Square, accum_out=ss[:, u:u + 1])
                last.then_inc(S["ss_ready"], 1)

            def m_yturn(b):
                for i, ps in ((1, M0), (2, M1)):
                    act.wait_ge(S["yT_ps"], nth(b, 2, i))
                    last = nc.scalar.copy(ygT[:, 2 * i - 2:2 * i, :], two(ps))
                last.then_inc(S["yT_ready"], 1)

            turns(nc.scalar, "scalar", dict(
                a_turn=evac_T("a", A0), g_turn=evac_T("g", Q0), m_turn=evac_T("m", M0),
                a_mlp1=a_mlp1, a_fcol=a_fcol, a_factors=a_factors, a_att=a_att, a_elu_b=a_elu_b, a_mlp2=a_mlp2,
                b_proj=proj("b", (A0, A2)), g_proj=proj("g", (Q0, Q1)),
                b_exp=softmax("b"), g_exp=softmax("g"), b_pturn=pturn("b", A2), g_pturn=pturn("g", Q1),
                b_att=elu_exp("b", A2), g_att=elu_exp("g", Q1), b_elu_b=b_elu_b,
                q_route=q_route, q_gather=q_gather, q_gelu_a=q_gelu_a, q_gelu_c=q_gelu_c,
                m_xbc_a=m_xbc_a, m_xbc_b=m_xbc_b, m_dt_exp=m_dt_exp, m_silu=m_silu, m_z=m_z,
                **parts("m_decay", m_decay, 2), m_xrow=m_xrow, m_gated=m_gated, m_yturn=m_yturn))

        @block.vector
        def _(v):
            def stats(k, src, ready):
                def step(b):
                    v.wait_ge(*((x_loaded, 16 * b) if ready is None else (S[ready], b)))
                    for u in range(U):
                        last = nc.vector.bn_stats(bn[k][:, u, :], src[:, u, :])
                    last.then_inc(S[f"{k}_stats"], 1)
                    v.wait_ge(S[f"{k}_stats"], nth(b, 2, 1))
                    nc.vector.memset(hold_cols[:, "aqgm".index(k):"aqgm".index(k) + 1], 0.0)
                    for u in range(U):
                        last = nc.vector.bn_aggr(mv[k][:, u, :], bn[k][:, u, :])
                    last.then_inc(S[f"{k}_stats"], 1)
                return step

            def norm(k, src):
                def step(b):
                    v.wait_ge(S[f"{k}_rstd"], nth(b, 2, 2))
                    for u in range(U):
                        last = nc.vector.tensor_scalar(xn[k][:, u, :], src[:, u, :], mv[k][:, u, 0:1],
                                                       rstd[k][:, u:u + 1], ALU.subtract, ALU.mult)
                    last.then_inc(S[f"{k}_xn"], 1)
                return step

            def a_fc(b):
                v.wait_ge(S["h1_ps"], nth(b, 2, 1))
                nc.vector.tensor_scalar(h1[:, :, 1, 0:D], two(A2), 1.0, None, ALU.add).then_inc(S["h1_b"], 1)

            def a_fcol(b):
                v.wait_ge(S["h1_ps"], nth(b, 2, 2))
                for u in range(U):
                    last = nc.vector.tensor_copy(f1[:, u, :], (A0, A1)[u][:, D:D + 2])
                last.then_inc(S["f1_ready"], 1)

            def a_maxima(b):
                v.wait_ge(S["fb_ps"], b)
                nc.vector.tensor_reduce(top[:], A2[:, N:2 * N], AX_X, ALU.max).then_inc(S["top_ready"], 1)
                v.wait_ge(S["top_ready"], b)
                nc.vector.tensor_scalar(arg[:], A2[:, 0:N], top[:, 0:1], 1.0 - ALPHA, ALU.add, ALU.mult)\
                    .then_inc(S["arg_ready"], 1)
                nc.vector.tensor_scalar(gcol[:], f1[:, :, 1], top[:, 0:1], None, ALU.subtract)\
                    .then_inc(S["gcol_ready"], 1)
                v.wait_ge(S["arg_ready"], b)
                nc.vector.tensor_scalar(args[:, 0, :], arg[:], 0.0, None, ALU.min)
                nc.vector.tensor_scalar(args[:, 1, :], arg[:], 0.0, -1.0, ALU.max, ALU.mult)\
                    .then_inc(S["args_ready"], 1)

            def a_probs(b):
                v.wait_ge(S["low_ready"], b)
                for u in range(U):
                    last = nc.vector.scalar_tensor_tensor(out=p1[:, u, :], in0=fac[:, 0, :], scalar=bcol[:, u:u + 1],
                                                          in1=low[:, u, :], op0=ALU.mult, op1=ALU.max)
                last.then_inc(S["p1_ready"], 1)

            def a_att(b):
                v.wait_ge(S["y1_ps"], nth(b, 2, 1))
                for u in range(U):
                    last = nc.vector.reciprocal(r1[:, u:u + 1], (A0, A1)[u][:, D:D + 1])
                last.then_inc(S["r1_ready"], 1)

            def a_elu_c(b):
                v.wait_ge(S["e1x_ready"], b)
                for u in range(U):
                    for half in range(H // D):
                        cols = slice(half * D, (half + 1) * D)
                        last = nc.vector.scalar_tensor_tensor(out=u1[:, u, cols], in0=rows1(half, u),
                                                              scalar=r1[:, u:u + 1], in1=e1x[:, u, cols],
                                                              op0=ALU.mult, op1=ALU.max)
                last.then_inc(S["u1_ready"], 1)

            def a_uturn(b):
                for i, ps, c in ((1, A2, 0), (2, A0, 2)):
                    v.wait_ge(S["u1T_ps"], nth(b, 2, i))
                    last = nc.vector.scalar_tensor_tensor(out=z1T[:, c:c + 2, :].rearrange("p c n -> p (c n)"), in0=ps[:, :],
                                                   scalar=-1.0, in1=o1T[:, c:c + 2, :].rearrange("p c n -> p (c n)"),
                                                          op0=ALU.add, op1=ALU.add)
                last.then_inc(S["z1_ready"], 1)

            def fcol(k, banks):
                def step(b):
                    v.wait_ge(S[f"{k}_h_ps"], b)
                    for u in range(U):
                        last = nc.vector.tensor_copy(fc[k][:, u, :], banks[u][:, D:D + 2])
                    last.then_inc(S[f"{k}_fc"], 1)
                return step

            def mask(k, ps, m):
                def step(b):
                    v.wait_ge(S[f"{k}_fb_ps"], b)
                    for u in range(U):
                        last = nc.vector.scalar_tensor_tensor(out=sc[k][:, u, :], in0=m[:, u, :],
                                                              scalar=fc[k][:, u, 0:1], in1=ps[:, N:2 * N],
                                                              op0=ALU.add, op1=ALU.add)
                    last.then_inc(S[f"{k}_sc"], 1)
                return step

            def lrelu(k):
                def step(b):
                    v.wait_ge(S[f"{k}_sc"], b)
                    nc.vector.scalar_tensor_tensor(out=lr[k][:], in0=sc[k][:], scalar=ALPHA, in1=sc[k][:],
                                                   op0=ALU.mult, op1=ALU.max).then_inc(S[f"{k}_lr"], 1)
                return step

            def rowmax(k):
                def step(b):
                    v.wait_ge(S[f"{k}_lr"], b)
                    nc.vector.tensor_reduce(nmax[k][:], lr[k][:], AX_X, ALU.max, negate=True)\
                        .then_inc(S[f"{k}_nmax"], 1)
                return step

            def rowsum(k):
                def step(b):
                    v.wait_ge(S[f"{k}_pr"], b)
                    nc.vector.reciprocal(rr[k][:], rs[k][:]).then_inc(S[f"{k}_rr"], 1)
                return step

            def elu_max(k, ps, e, ready):
                def step(b):
                    v.wait_ge(S[ready], b)
                    for u in range(U):
                        last = nc.vector.scalar_tensor_tensor(out=ue[k][:, u, :], in0=two(ps)[:, u, :],
                                                              scalar=rr[k][:, u:u + 1], in1=e[:, u, :],
                                                              op0=ALU.mult, op1=ALU.max)
                    last.then_inc(S[f"{k}_ue"], 1)
                return step

            def b_x1(b):
                v.wait_ge(S["b_ue"], b)
                v.wait_ge(S["res_ps"], b)
                nc.vector.scalar_tensor_tensor(out=v1[:, :, :].rearrange("p u d -> p (u d)"), in0=A1[:, :], scalar=-1.0,
                                               in1=ue["b"][:, :, :].rearrange("p u d -> p (u d)"), op0=ALU.add,
                                               op1=ALU.add).then_inc(S["v1_ready"], 1)
                v.wait_ge(S["v1_ready"], b)
                v.wait_ge(x0_loaded, 16 * b)
                before(v, S["xs_ready"], b)
                nc.vector.scalar_tensor_tensor(out=x1[:], in0=v1[:], scalar=0.0, in1=x0[:], op0=ALU.max, op1=ALU.add)\
                    .then_inc(S["x1_ready"], 1)

            def g_x3(b):
                v.wait_ge(S["g_ue"], b)
                before(v, S["x3b_ready"], b)
                nc.vector.scalar_tensor_tensor(out=x3[:], in0=ue["g"][:], scalar=-1.0, in1=x2[:], op0=ALU.add,
                                               op1=ALU.add).then_inc(S["x3_ready"], 1)

            def q_route(b):
                v.wait_ge(S["q_xn"], b)
                for u in range(U):
                    last = nc.vector.scalar_tensor_tensor(out=(junk, wrow)[u][:], in0=xn["q"][:, u, :], scalar=1.0,
                                                          in1=w_route[:], op0=ALU.mult, op1=ALU.mult,
                                                          accum_out=wsum[:, u:u + 1])
                last.then_inc(S["wsum_ready"], 1)

            def q_route_col(b):
                v.wait_ge(S["wrow_ready"], b)
                for u in range(U):
                    last = nc.vector.scalar_tensor_tensor(out=junk[:, u * P:(u + 1) * P], in0=wrow[:, u * P:(u + 1) * P],
                                                          scalar=1.0, in1=ident[:], op0=ALU.mult, op1=ALU.mult,
                                                          accum_out=wcol[:, u:u + 1])
                last.then_inc(S["wcol_ready"], 1)

            def q_rank(b):
                v.wait_ge(S["wcol_ready"], b)
                spare = gsq[:, :, :].rearrange("p (a c) r -> p a (c r)", a=4)
                for u in range(U):
                    nc.vector.tensor_scalar(spare[:, 2 * u, :], wrow[:], wcol[:, u:u + 1], None,
                                            ALU.is_gt, ALU.add, accum_out=above[:, u:u + 1])
                    last = nc.vector.scalar_tensor_tensor(out=spare[:, 2 * u + 1, :], in0=wrow[:],
                                                          scalar=wcol[:, u:u + 1], in1=earlier[:, u, :],
                                                          op0=ALU.is_equal, op1=ALU.mult,
                                                          accum_out=ties[:, u:u + 1])
                last.then_inc(S["counts_ready"], 1)
                v.wait_ge(S["counts_ready"], b)
                nc.vector.tensor_tensor(rank[:], above[:], ties[:], ALU.add).then_inc(S["rank_ready"], 1)
                v.wait_ge(S["rank_ready"], b)
                for u in range(U):
                    last = nc.vector.tensor_scalar(pick[:, u, :], slot[:], rank[:, u:u + 1], None, ALU.is_equal)
                last.then_inc(S["pick_ready"], 1)

            def q_gelu_a(b):
                for i, ps, k in ((1, Q0, 0), (2, Q1, KF // 2)):
                    v.wait_ge(S["up_ps"], nth(b, 2, i))
                    last = nc.vector.tensor_tensor(ga_[:, k:k + KF // 2, :], ps[:, :].rearrange("p (k r) -> p k r", r=P),
                                                   c_up[:, k:k + KF // 2, None].to_broadcast([P, KF // 2, P]), ALU.add)
                last.then_inc(S["ga_ready"], 1)

            def q_gelu_b(b):
                v.wait_ge(S["gpl_ready"], b)
                nc.vector.tensor_tensor(gq[:], gpl[:], ga_[:], ALU.mult).then_inc(S["gq_ready"], 1)

            def q_ffn2(b):
                v.wait_ge(S["gt_ready"], b)
                nc.vector.scalar_tensor_tensor(out=gl[:], in0=gt[:], scalar=1.0, in1=ga_[:], op0=ALU.add, op1=ALU.mult)\
                    .then_inc(S["gl_ready"], 1)

            def q_scatter(b):
                v.wait_ge(S["yff_ps"], b)
                nc.vector.tensor_tensor(yff[:], Q0[:, 0:D], c_down[:], ALU.add).then_inc(S["yff_ready"], 1)

            def q_x2(b):
                v.wait_ge(S["sc_ps"], b)
                v.wait_ge(S["xs_ready"], b)
                for u in range(U):
                    last = nc.vector.scalar_tensor_tensor(out=x2[:, u, :], in0=two(Q1)[:, u, :], scalar=wcol[:, u:u + 1],
                                                          in1=xs[:, u, :], op0=ALU.mult, op1=ALU.add)
                last.then_inc(S["x2_ready"], 1)

            def m_conv_b(b, i):
                if i == 0:
                    v.wait_ge(S["acc_ready"], b)
                else:
                    v.wait_ge(S["conv"], nth(b, 3, i))
                tap = PAD - 1 - i
                for k in range(KX):
                    last = nc.vector.scalar_tensor_tensor(out=acc[:, k, :], in0=xbc[:, k, tap:tap + N],
                                                          scalar=w_conv[:, k, tap:tap + 1], in1=acc[:, k, :],
                                                          op0=ALU.mult, op1=ALU.add)
                last.then_inc(S["conv"], 1)

            def m_silu(b):
                v.wait_ge(S["th_ready"], b)
                c = acc
                nc.vector.scalar_tensor_tensor(out=xc[:, 0:KI, :], in0=th[:, 0:KI, :], scalar=1.0, in1=c[:, 0:KI, :],
                                               op0=ALU.add, op1=ALU.mult)
                nc.vector.scalar_tensor_tensor(out=bT[:], in0=th[0:DS, KI, :], scalar=1.0, in1=c[0:DS, KI, :],
                                               op0=ALU.add, op1=ALU.mult)
                nc.vector.scalar_tensor_tensor(out=cT[:], in0=th[DS:, KI, :], scalar=1.0, in1=c[DS:, KI, :],
                                               op0=ALU.add, op1=ALU.mult).then_inc(S["xc_ready"], 1)

            def m_scan(b):
                v.wait_ge(S["dA_ps"], b)
                nc.vector.tensor_tensor_scan(cumT[0:NH, :], ones[0:NH, :], M1[0:NH, 0:N], 0.0, ALU.mult, ALU.add)\
                    .then_inc(S["cumT_ready"], 1)

            def m_cum_col(b):
                v.wait_ge(S["cumc_ps"], b)
                nc.vector.tensor_copy(cumcol[:], M1[:, 0:U * P].rearrange("p (u h) -> p u h", u=U)[:, :, 0:NH])\
                    .then_inc(S["cumcol_ready"], 1)

            def m_cb(b):
                v.wait_ge(S["cb_ps"], b)
                nc.vector.tensor_tensor(cb[:], M1[:, 0:N + P], causal[:], ALU.mult).then_inc(S["cb_ready"], 1)

            def m_gate(b):
                for i, (cols, z) in enumerate(((tz[:, 0, 0:D], M1[:, 0:D]), (tz[:, 1, 0:D], M0[:, 0:D]),
                                               (tz[:, :, D:], two(M2)))):
                    v.wait_ge(S["tz_ready"], nth(b, 3, i + 1))
                    nc.vector.scalar_tensor_tensor(out=cols, in0=cols, scalar=1.0, in1=z, op0=ALU.add,
                                                   op1=ALU.mult).then_inc(S["gz_ready"], 1)

            def m_mix(b, i):
                v.wait_ge(S["dec_ready"], nth(b, 2, i + 1))
                v.wait_ge(S["cb_ready"], b)
                dec, c_b = ((dec0, cb[:, None, 0:N]), (dec1, cb[:, None, N:]))[i]
                nc.vector.tensor_tensor(dec[:], dec[:], c_b.to_broadcast([P, NH, c_b.shape[-1]]), ALU.mult)\
                    .then_inc(S["mix_ready"], 1)

            def m_decay(b, i):
                v.wait_ge(S["cumcol_ready"], b)
                v.wait_ge(cum_spread, 16 * b)
                dec, columns = ((dec0, cumB), (dec1, cumB[:, :, P:]))[i]
                for h in range(NH):
                    last = nc.vector.tensor_scalar(dec[:, h, :], columns[:, h, :], cumcol[:, i, h:h + 1], 0.0,
                                                   ALU.subtract, ALU.min)
                last.then_inc(S["decarg_ready"], 1)

            def m_y(b, u):
                v.wait_ge(S["dx_ready"], b)
                v.wait_ge(S["y_ps"], nth(b, 2, u + 1))
                nc.vector.tensor_tensor(xr[:, u, :], (M1, M2)[u][:, :], xr[:, u, :], ALU.add)\
                    .then_inc(S["ysum"], 1)
                v.wait_ge(S["ysum"], nth(b, 2, u + 1))
                nc.vector.tensor_tensor(yg[:, u, :], xr[:, u, :], gz[:, u, :], ALU.mult)\
                    .then_inc(S["yg_ready"], 1)

            def m_out(b):
                v.wait_ge(S["out_ps"], b)
                v.wait_ge(S["rms_ready"], nth(b, 2, 2))
                v.wait_ge(S["x3b_ready"], b)
                for u in range(U):
                    last = nc.vector.scalar_tensor_tensor(out=x4[:, u, :], in0=two(M2)[:, u, :], scalar=rms[:, u:u + 1],
                                                          in1=x3b[:, u, :], op0=ALU.mult, op1=ALU.add)
                last.then_inc(S["x4_ready"], 1)

            turns(nc.vector, "vector", dict(
                a_stats=stats("a", x_in, None), q_stats=stats("q", x1, "x1_ready"),
                g_stats=stats("g", x2, "x2_ready"), m_stats=stats("m", x3, "x3_ready"),
                a_norm=norm("a", x_in), q_norm=norm("q", x1), g_norm=norm("g", x2), m_norm=norm("m", x3),
                a_fc=a_fc, a_fcol=a_fcol, a_maxima=a_maxima, a_probs=a_probs, a_att=a_att, a_elu_c=a_elu_c,
                a_uturn=a_uturn, b_proj=fcol("b", (A0, A2)), g_proj=fcol("g", (Q0, Q1)), b_mask=mask("b", A0, mask0),
                g_mask=mask("g", Q0, mask1), b_lrelu=lrelu("b"), g_lrelu=lrelu("g"),
                b_max=rowmax("b"), g_max=rowmax("g"), b_pturn=rowsum("b"),
                g_pturn=rowsum("g"), b_elu_c=elu_max("b", A2, ec, "b_ec"), g_elu_b=elu_max("g", Q1, eb["g"], "g_eb"),
                b_x1=b_x1, g_x3=g_x3, q_route=q_route, q_route_col=q_route_col, q_rank=q_rank,
                q_gelu_a=q_gelu_a, q_gelu_b=q_gelu_b,
                q_ffn2=q_ffn2, q_scatter=q_scatter, q_x2=q_x2, **parts("m_conv_b", m_conv_b, PAD), m_silu=m_silu,
                m_scan=m_scan,
                m_cum_col=m_cum_col, m_cb=m_cb, m_gate=m_gate, **parts("m_decay", m_decay, 2),
                **parts("m_mix", m_mix, 2), **parts("m_y", m_y, U), m_out=m_out))

        @block.tensor
        def _(pe):
            def spread_column(row, column):
                return nc.tensor.transpose(row, column.to_broadcast([P, P]), ident[:])

            def turn_rows(k, ps, freed=None):
                def step(b):
                    pe.wait_ge(S[f"{k}_xn"], b)
                    if freed is not None:
                        before(pe, S[freed], b)
                    for c in range(KD):
                        for u in range(U):
                            last = nc.tensor.transpose(ps[:, c * N + u * P:c * N + (u + 1) * P],
                                                       xn[k][:, u, c * P:(c + 1) * P], ident[:])
                    last.then_inc(S[f"{k}_xT_ps"], 1)
                return step

            def a_mlp1(b, i):
                pe.wait_ge(S["a_xT"], b)
                before(pe, S[("v1_ready", "b_ue")[i]], b)
                ps, m0 = ((A1, 0), (A2, 2))[i]
                for m in (m0, m0 + 1):
                    for k in range(KD):
                        last = nc.tensor.matmul(ps[:, (m - m0) * N:(m - m0 + 1) * N],
                                                w_mlp1[:, k, m * P:(m + 1) * P], xT["a"][:, k, :],
                                                start=(k == 0), stop=(k == KD - 1))
                last.then_inc(S["o1_ps"], 1)

            def a_fc(b, i):
                pe.wait_ge(S["o1_ready"], b)
                half = 1 - i
                for u in range(U):
                    for k in range(KH):
                        last = nc.tensor.matmul(rows1(half, u, 2), o1T[:, k, u * P:(u + 1) * P],
                                                w_fc[:, k, half, 0:D + 2 * i],
                                                start=(k == 0), stop=(k == KH - 1))
                last.then_inc(S["h1_ps"], 1)

            def a_bcast(b):
                pe.wait_ge(S["f1_ready"], b)
                pe.wait_ge(S["h1_b"], b)
                for half in range(2):
                    for u in range(U):
                        last = spread_column(A2[:, half * N + u * P:half * N + (u + 1) * P], f1[:, u, half:half + 1])
                last.then_inc(S["fb_ps"], 1)

            def a_att(b, half):
                pe.wait_ge(S["p1_ready"], b)
                pe.wait_ge(S[("h1_a", "h1_b")[half]], b)
                for u in range(U):
                    for j in range(U):
                        last = nc.tensor.matmul(rows1(half, u, 1), p1[:, j, u * P:(u + 1) * P],
                                                h1[:, j, half, 0:D + 1 - half],
                                                start=(j == 0), stop=(j == U - 1))
                last.then_inc(S["y1_ps"], 1)

            def a_uturn(b):
                pe.wait_ge(S["u1_ready"], b)
                for ps, c0 in ((A2, 0), (A0, 2)):
                    for c in (c0, c0 + 1):
                        for u in range(U):
                            last = nc.tensor.transpose(ps[:, (c - c0) * N + u * P:(c - c0) * N + (u + 1) * P],
                                                       u1[:, u, c * P:(c + 1) * P], ident[:])
                    last.then_inc(S["u1T_ps"], 1)

            def a_mlp2(b):
                pe.wait_ge(S["z1_ready"], b)
                for m in range(KD):
                    for k in range(KH):
                        last = nc.tensor.matmul(A1[:, m * N:(m + 1) * N], w_mlp2[:, k, m * P:(m + 1) * P],
                                                z1T[:, k, :], start=(k == 0), stop=(k == KH - 1))
                last.then_inc(S["o2_ps"], 1)

            def proj(k, ready, src, w, banks):
                def step(b):
                    pe.wait_ge(S[ready], b)
                    for u in range(U):
                        for c in range(KD):
                            last = nc.tensor.matmul(banks[u][:, 0:D + 2], src[:, c, u * P:(u + 1) * P], w[:, c, :],
                                                    start=(c == 0), stop=(c == KD - 1))
                    last.then_inc(S[f"{k}_h_ps"], 1)
                return step

            def bcast(k, ps):
                def step(b):
                    pe.wait_ge(S[f"{k}_hp"], b)
                    for u in range(U):
                        last = spread_column(ps[:, N + u * P:N + (u + 1) * P], fc[k][:, u, 1:2])
                    last.then_inc(S[f"{k}_fb_ps"], 1)
                return step

            def b_res(b):
                pe.wait_ge(S["o2_ready"], b)
                for u in range(U):
                    for c in range(KD):
                        last = nc.tensor.transpose(A1[:, u * D + c * P:u * D + (c + 1) * P],
                                                   o2T[:, c, u * P:(u + 1) * P], ident[:])
                last.then_inc(S["res_ps"], 1)

            def pturn(k, ps):
                def step(b):
                    pe.wait_ge(S[f"{k}_pr"], b)
                    for j in range(U):
                        for u in range(U):
                            last = nc.tensor.transpose(ps[:, j * N + u * P:j * N + (u + 1) * P],
                                                       pr[k][:, u, j * P:(j + 1) * P], ident[:])
                    last.then_inc(S[f"{k}_pT_ps"], 1)
                return step

            def att(k, ps):
                def step(b):
                    pe.wait_ge(S[f"{k}_pT"], b)
                    pe.wait_ge(S[f"{k}_hp"], b)
                    for u in range(U):
                        for j in range(U):
                            last = nc.tensor.matmul(ps[:, u * D:(u + 1) * D], pT[k][:, j, u * P:(u + 1) * P],
                                                    hp[k][:, j, :], start=(j == 0), stop=(j == U - 1))
                    last.then_inc(S[f"{k}_y_ps"], 1)
                return step

            def q_route(b):
                pe.wait_ge(S["wsum_ready"], b)
                before(pe, S["g_sc"], b)
                for u in range(U):
                    last = spread_column(Q0[:, u * P:(u + 1) * P], wsum[:, u:u + 1])
                last.then_inc(S["w_ps"], 1)

            def q_gather(b):
                pe.wait_ge(S["pick_ready"], b)
                for u in range(U):
                    nc.tensor.transpose(Q0[:, u * P:(u + 1) * P], pick[:, u, :], ident[:])
                for c in range(KD):
                    for u in range(U):
                        last = nc.tensor.matmul(Q0[:, N + c * P:N + (c + 1) * P], xn["q"][:, u, c * P:(c + 1) * P],
                                                pick[:, u, :], start=(u == 0), stop=(u == U - 1))
                last.then_inc(S["sel_ps"], 1)

            def q_ffn1(b, i):
                pe.wait_ge(S["sel_ready"], b)
                if i:
                    before(pe, S["g_ue"], b)
                ps, m0 = ((Q0, 0), (Q1, KF // 2))[i]
                for m in range(m0, m0 + KF // 2):
                    for c in range(KD):
                        last = nc.tensor.matmul(ps[:, (m - m0) * P:(m - m0 + 1) * P], w_up[:, c, m * P:(m + 1) * P],
                                                selT[:, c, :], start=(c == 0), stop=(c == KD - 1))
                last.then_inc(S["up_ps"], 1)

            def q_ffn2(b):
                pe.wait_ge(S["gl_ready"], b)
                for m in range(KF):
                    last = nc.tensor.matmul(Q0[:, 0:D], gl[:, m, :], w_down[:, m, :], start=(m == 0), stop=(m == KF - 1))
                last.then_inc(S["yff_ps"], 1)

            def q_scatter(b):
                pe.wait_ge(S["yff_ready"], b)
                for u in range(U):
                    last = nc.tensor.matmul(Q1[:, u * D:(u + 1) * D], pickT[:, u * P:(u + 1) * P], yff[:],
                                            start=True, stop=True)
                last.then_inc(S["sc_ps"], 1)

            def xbc_tile(ps, at, k):
                for c in range(KD):
                    last = nc.tensor.matmul(ps[:, at:at + N], w_in[:, c, X0 + k * P:X0 + (k + 1) * P], xT["m"][:, c, :],
                                            start=(c == 0), stop=(c == KD - 1))
                return last

            def m_xbc_a(b):
                pe.wait_ge(S["gz_ready"], nth(b, 3, 1))
                xbc_tile(M1, N, 4).then_inc(S["xbc_ps"], 1)
                pe.wait_ge(S["gz_ready"], nth(b, 3, 3))
                xbc_tile(M2, 0, 0)
                xbc_tile(M2, N, 1).then_inc(S["xbc_ps"], 1)

            def m_xbc_b(b):
                xbc_tile(M0, 0, 2)
                xbc_tile(M0, N, 3).then_inc(S["xbc_ps"], 1)

            def m_z(b):
                pe.wait_ge(S["m_xT"], b)
                for u in range(U):
                    for c in range(KD):
                        last = nc.tensor.matmul((M1, M0)[u][:, 0:D + NH], xT["m"][:, c, u * P:(u + 1) * P],
                                                w_in[:, c, Z0:Z0 + D + NH], start=(c == 0), stop=(c == KD - 1))
                    last.then_inc(S["z_ps"], 1)
                before(pe, S["x4_ready"], b)
                for u in range(U):
                    for c in range(KD):
                        last = nc.tensor.matmul(M2[:, u * D:(u + 1) * D], xT["m"][:, c, u * P:(u + 1) * P],
                                                w_in[:, c, Z1:Z1 + DI - D], start=(c == 0), stop=(c == KD - 1))
                last.then_inc(S["z_ps"], 1)

            def m_da(b):
                pe.wait_ge(S["da_ready"], b)
                pe.wait_ge(S["xbc_ready"], nth(b, 3, 1))
                for u in range(U):
                    last = nc.tensor.transpose(M1[0:NH, u * P:(u + 1) * P], dA[:, u, :], ident[:])
                last.then_inc(S["dA_ps"], 1)

            def m_cum_col(b):
                pe.wait_ge(S["cumT_ready"], b)
                for u in range(U):
                    last = nc.tensor.transpose(M1[:, u * P:(u + 1) * P], cumT[:, u * P:(u + 1) * P], ident[:])
                last.then_inc(S["cumc_ps"], 1)

            def m_cb(b):
                pe.wait_ge(S["xc_ready"], b)
                pe.wait_ge(S["cumcol_ready"], b)
                nc.tensor.matmul(M1[:, 0:N], bT[:, 0:P], cT[:, :], start=True, stop=True)
                nc.tensor.matmul(M1[:, N:N + P], bT[:, P:], cT[:, P:], start=True, stop=True).then_inc(S["cb_ps"], 1)

            def m_xrow(b):
                pe.wait_ge(S["xc_ready"], b)
                for u in range(U):
                    pe.wait_ge(S["xbc_ready"], nth(b, 3, u + 2))
                    for c in range(KI):
                        last = nc.tensor.transpose((M2, M0)[u][:, c * P:(c + 1) * P], xc[:, c, u * P:(u + 1) * P],
                                                   ident[:])
                    last.then_inc(S["xr_ps"], 1)

            def m_y(b, u):
                pe.wait_ge(S["mix_ready"], nth(b, 2, u + 1))
                pe.wait_ge(S["xdt_ready"], b)
                for h in range(NH):
                    for s in range(u + 1):
                        lhsT = dec0[:, h, u * P:(u + 1) * P] if s == 0 else dec1[:, h, :]
                        last = nc.tensor.matmul((M1, M2)[u][:, h * HD:(h + 1) * HD], lhsT,
                                                xdt[:, s, h * HD:(h + 1) * HD], start=(s == 0), stop=(s == u))
                last.then_inc(S["y_ps"], 1)

            def m_yturn(b):
                pe.wait_ge(S["yg_ready"], nth(b, 2, 2))
                for ps, c0 in ((M0, 0), (M1, 2)):
                    for c in (c0, c0 + 1):
                        for u in range(U):
                            last = nc.tensor.transpose(ps[:, (c - c0) * N + u * P:(c - c0) * N + (u + 1) * P],
                                                       yg[:, u, c * P:(c + 1) * P], ident[:])
                    last.then_inc(S["yT_ps"], 1)

            def m_out(b):
                pe.wait_ge(S["yT_ready"], b)
                for u in range(U):
                    for c in range(KI):
                        last = nc.tensor.matmul(M2[:, u * D:(u + 1) * D], ygT[:, c, u * P:(u + 1) * P], w_comb[:, c, :],
                                                start=(c == 0), stop=(c == KI - 1))
                last.then_inc(S["out_ps"], 1)

            turns(nc.tensor, "tensor", dict(
                a_turn=turn_rows("a", A0, "b_sc"), g_turn=turn_rows("g", Q0),
                m_turn=turn_rows("m", M0, "yT_ready"), **parts("a_mlp1", a_mlp1, 2), **parts("a_fc", a_fc, 2),
                a_bcast=a_bcast, **parts("a_att", a_att, H // D), a_uturn=a_uturn,
                a_mlp2=a_mlp2, b_proj=proj("b", "o2_ready", o2T, w_hand, (A0, A2)),
                g_proj=proj("g", "g_xT", xT["g"], w_gat, (Q0, Q1)), b_res=b_res, b_bcast=bcast("b", A0),
                g_bcast=bcast("g", Q0), b_pturn=pturn("b", A2), g_pturn=pturn("g", Q1), b_att=att("b", A2),
                g_att=att("g", Q1), q_route=q_route, q_gather=q_gather, **parts("q_ffn1", q_ffn1, 2),
                q_ffn2=q_ffn2, q_scatter=q_scatter, m_xbc_a=m_xbc_a, m_xbc_b=m_xbc_b, m_z=m_z, m_da=m_da,
                m_cum_col=m_cum_col, m_cb=m_cb, m_xrow=m_xrow, **parts("m_y", m_y, U), m_yturn=m_yturn, m_out=m_out))


_INS = ["x", "adj", "L0_gnn_mlp1_w", "L0_gnn_mlp1_b", "L0_gnn_mlp2_w", "L0_gnn_mlp2_b", "L0_gnn_W_fc", "L0_gnn_a_fc",
        "L0_gnn_W_hand", "L0_gnn_a_hand", "L0_ffn_wr", "L0_ffn_br", "L0_ffn_w1", "L0_ffn_b1", "L0_ffn_w2", "L0_ffn_b2",
        "L1_gnn_W", "L1_gnn_a", "L1_ffn_W_in", "L1_ffn_conv_w", "L1_ffn_conv_b", "L1_ffn_dt_bias", "L1_ffn_A_log",
        "L1_ffn_D", "L1_ffn_norm_w", "L1_ffn_W_out", "L1_ffn_W_lin", "L1_ffn_b_lin"]


def kernel(**inputs):
    import numpy as _np
    import concourse.bacc as _bacc
    from concourse import mybir as _mybir
    from concourse.bass_utils import run_bass_kernel_spmd as _run

    nc = _bacc.Bacc("TRN2", target_bir_lowering=False, num_devices=1)
    arrays, args = {}, []
    for name in _INS:
        a = _np.ascontiguousarray(inputs[name])
        arrays[f"in_{name}"] = a
        args.append(nc.dram_tensor(f"in_{name}", a.shape, _mybir.dt.from_np(a.dtype), kind="ExternalInput").ap())
    args.append(nc.dram_tensor("out_0", inputs["x"].shape, F32, kind="ExternalOutput").ap())
    gnn_ffn_mamba_kernel(nc, *args)
    r = _run(nc, [arrays], core_ids=[0])
    return r.results[0]["out_0"]
```
